# Optimizing a Trainium2 kernel written in Bass

```python
import numpy as np
import jax
import jax.numpy as jnp

def _softmax(x, axis=-1):
    return jax.nn.softmax(x, axis=axis)

def _gelu(x):
    return jax.nn.gelu(x, approximate=True)

def _silu(x):
    return jax.nn.silu(x)

def _sigmoid(x):
    return jax.nn.sigmoid(x)

def _layernorm(x, axis=-1, eps=1e-05):
    m = jnp.mean(x, axis=axis, keepdims=True)
    v = jnp.var(x, axis=axis, keepdims=True)
    return (x - m) / jnp.sqrt(v + eps)

def _scatter_add(tgt, idx, src, axis=0):
    return tgt.at[idx].add(src)

def _segment_sum(src, seg, n):
    return jax.ops.segment_sum(src, seg, n)
kernel_name = 'mk_macaron_d1_jaxref_r8_b66e17'

def setup_inputs(seed: int=0):
    np.random.seed(seed)
    _w = jnp.asarray

    def _L0_attn_setup():
        import jax, jax.numpy as jnp
        import numpy as np
        D_MODEL, N_HEADS, D_FF = (128, 16, 512)
        SCALE = 0.1
        NUM_BITS = 8
        LEVELS = 1 << NUM_BITS
        HALF = LEVELS // 2
        MAX_EXP = 4
        EPS = 1e-05

        def pow2_weight(key, shape, max_exp=MAX_EXP):
            k1, k2 = jax.random.split(key)
            sign = jax.random.randint(k1, shape, -1, 2).astype(jnp.float32)
            e = jax.random.randint(k2, shape, max_exp, max_exp + 4).astype(jnp.float32)
            return sign * jnp.exp2(-e)

        def _layernorm(x, g, b):
            mu = jnp.mean(x, axis=-1, keepdims=True)
            var = jnp.var(x, axis=-1, keepdims=True)
            return (x - mu) * jax.lax.rsqrt(var + EPS) * g + b

        def _lookup_act(x):
            grid = (jnp.arange(LEVELS, dtype=jnp.float32) - HALF) * SCALE
            table = jax.nn.gelu(grid)
            idx = jnp.clip(jnp.round(x / SCALE).astype(jnp.int32) + HALF, 0, LEVELS - 1)
            return table[idx]

        def _linear_attention(x, wq, wk, wv, wo):
            B, S, D = x.shape
            H, Dh = (N_HEADS, D // N_HEADS)
            q = (x @ wq).reshape(B, S, H, Dh)
            k = (x @ wk).reshape(B, S, H, Dh)
            v = (x @ wv).reshape(B, S, H, Dh)
            phi_q = jax.nn.elu(q) + 1.0
            phi_k = jax.nn.elu(k) + 1.0
            kv = jnp.einsum('bshd,bshe->bhde', phi_k, v)
            z = jnp.sum(phi_k, axis=1)
            num = jnp.einsum('bshd,bhde->bshe', phi_q, kv)
            den = jnp.einsum('bshd,bhd->bsh', phi_q, z)[..., None] + 1e-06
            out = (num / den).reshape(B, S, D)
            return out @ wo
        key = jax.random.key(seed)
        ks = jax.random.split(key, 8)
        x = jax.random.normal(ks[0], (4, 256, D_MODEL), dtype=jnp.float32)
        return {'x': x, 'ln1_g': jnp.ones((D_MODEL,), jnp.float32), 'ln1_b': jnp.zeros((D_MODEL,), jnp.float32), 'wq': pow2_weight(ks[1], (D_MODEL, D_MODEL)), 'wk': pow2_weight(ks[2], (D_MODEL, D_MODEL)), 'wv': pow2_weight(ks[3], (D_MODEL, D_MODEL)), 'wo': pow2_weight(ks[4], (D_MODEL, D_MODEL)), 'ln2_g': jnp.ones((D_MODEL,), jnp.float32), 'ln2_b': jnp.zeros((D_MODEL,), jnp.float32), 'w1': pow2_weight(ks[5], (D_MODEL, D_FF)), 'w2': pow2_weight(ks[6], (D_FF, D_MODEL))}
    _L0_attn_in = _L0_attn_setup()

    def _L0_ffn_setup():
        import jax, jax.numpy as jnp
        import numpy as np
        D_MODEL = 128
        D_FF = 512
        N_EXPERTS = 8
        INIT_SCALE = 0.1

        def _trunc_normal(key, shape, std):
            return std * jax.random.truncated_normal(key, -2.0, 2.0, shape, dtype=jnp.float32)
        key = jax.random.key(seed)
        ks = jax.random.split(key, 5)
        x = jax.random.normal(ks[0], (4, 128, D_MODEL), dtype=jnp.float32)
        router_W = _trunc_normal(ks[1], (D_MODEL, N_EXPERTS), INIT_SCALE / np.sqrt(D_MODEL))
        router_b = jnp.zeros((N_EXPERTS,), dtype=jnp.float32)
        W1 = _trunc_normal(ks[2], (N_EXPERTS, D_MODEL, D_FF), INIT_SCALE / np.sqrt(D_MODEL))
        b1 = jnp.zeros((N_EXPERTS, D_FF), dtype=jnp.float32)
        W2 = _trunc_normal(ks[3], (N_EXPERTS, D_FF, D_MODEL), INIT_SCALE / np.sqrt(D_FF))
        b2 = jnp.zeros((N_EXPERTS, D_MODEL), dtype=jnp.float32)
        return {'x': x, 'router_W': router_W, 'router_b': router_b, 'W1': W1, 'b1': b1, 'W2': W2, 'b2': b2}
    _L0_ffn_in = _L0_ffn_setup()
    _d = {'L0_attn_x': _L0_attn_in['x'], 'L0_attn_ln1_g': _L0_attn_in['ln1_g'], 'L0_attn_ln1_b': _L0_attn_in['ln1_b'], 'L0_attn_wq': _L0_attn_in['wq'], 'L0_attn_wk': _L0_attn_in['wk'], 'L0_attn_wv': _L0_attn_in['wv'], 'L0_attn_wo': _L0_attn_in['wo'], 'L0_attn_ln2_g': _L0_attn_in['ln2_g'], 'L0_attn_ln2_b': _L0_attn_in['ln2_b'], 'L0_attn_w1': _L0_attn_in['w1'], 'L0_attn_w2': _L0_attn_in['w2'], 'L0_ffn_router_W': _L0_ffn_in['router_W'], 'L0_ffn_router_b': _L0_ffn_in['router_b'], 'L0_ffn_W1': _L0_ffn_in['W1'], 'L0_ffn_b1': _L0_ffn_in['b1'], 'L0_ffn_W2': _L0_ffn_in['W2'], 'L0_ffn_b2': _L0_ffn_in['b2']}
    _x0 = _d['L0_attn_x']
    _d['L0_attn_x'] = jax.random.normal(jax.random.fold_in(jax.random.key(seed), 1), (4, 512, 128), dtype=_x0.dtype)
    del _x0
    return _d

def reference(L0_attn_x, L0_attn_ln1_g, L0_attn_ln1_b, L0_attn_wq, L0_attn_wk, L0_attn_wv, L0_attn_wo, L0_attn_ln2_g, L0_attn_ln2_b, L0_attn_w1, L0_attn_w2, L0_ffn_router_W, L0_ffn_router_b, L0_ffn_W1, L0_ffn_b1, L0_ffn_W2, L0_ffn_b2):

    def _L0_attn_ref(x, ln1_g, ln1_b, wq, wk, wv, wo, ln2_g, ln2_b, w1, w2):
        import jax, jax.numpy as jnp
        import numpy as np
        D_MODEL, N_HEADS, D_FF = (128, 16, 512)
        SCALE = 0.1
        NUM_BITS = 8
        LEVELS = 1 << NUM_BITS
        HALF = LEVELS // 2
        MAX_EXP = 4
        EPS = 1e-05

        def pow2_weight(key, shape, max_exp=MAX_EXP):
            k1, k2 = jax.random.split(key)
            sign = jax.random.randint(k1, shape, -1, 2).astype(jnp.float32)
            e = jax.random.randint(k2, shape, max_exp, max_exp + 4).astype(jnp.float32)
            return sign * jnp.exp2(-e)

        def _layernorm(x, g, b):
            mu = jnp.mean(x, axis=-1, keepdims=True)
            var = jnp.var(x, axis=-1, keepdims=True)
            return (x - mu) * jax.lax.rsqrt(var + EPS) * g + b

        def _lookup_act(x):
            grid = (jnp.arange(LEVELS, dtype=jnp.float32) - HALF) * SCALE
            table = jax.nn.gelu(grid)
            idx = jnp.clip(jnp.round(x / SCALE).astype(jnp.int32) + HALF, 0, LEVELS - 1)
            return table[idx]

        def _linear_attention(x, wq, wk, wv, wo):
            B, S, D = x.shape
            H, Dh = (N_HEADS, D // N_HEADS)
            q = (x @ wq).reshape(B, S, H, Dh)
            k = (x @ wk).reshape(B, S, H, Dh)
            v = (x @ wv).reshape(B, S, H, Dh)
            phi_q = jax.nn.elu(q) + 1.0
            phi_k = jax.nn.elu(k) + 1.0
            kv = jnp.einsum('bshd,bshe->bhde', phi_k, v)
            z = jnp.sum(phi_k, axis=1)
            num = jnp.einsum('bshd,bhde->bshe', phi_q, kv)
            den = jnp.einsum('bshd,bhd->bsh', phi_q, z)[..., None] + 1e-06
            out = (num / den).reshape(B, S, D)
            return out @ wo
        x = x + _linear_attention(_layernorm(x, ln1_g, ln1_b), wq, wk, wv, wo)
        h = _layernorm(x, ln2_g, ln2_b)
        x = x + _lookup_act(h @ w1) @ w2
        return x

    def _L0_ffn_ref(x, router_W, router_b, W1, b1, W2, b2):
        import jax, jax.numpy as jnp
        import numpy as np
        D_MODEL = 128
        D_FF = 512
        N_EXPERTS = 8
        INIT_SCALE = 0.1

        def _trunc_normal(key, shape, std):
            return std * jax.random.truncated_normal(key, -2.0, 2.0, shape, dtype=jnp.float32)
        logits = jnp.einsum('bsd,de->bse', x.astype(jnp.float32), router_W) + router_b
        probs = jax.nn.softmax(logits, axis=-1)
        top1 = jnp.argmax(probs, axis=-1)
        mask = jax.nn.one_hot(top1, N_EXPERTS, dtype=x.dtype)
        gates = mask * probs.astype(x.dtype)
        h = jax.nn.relu(jnp.einsum('bsd,edf->besf', x, W1) + b1[:, None, :])
        y = jnp.einsum('besf,efd->besd', h, W2) + b2[:, None, :]
        out = jnp.einsum('bse,besd->bsd', gates, y)
        return out
    x = L0_attn_x
    x = x + 0.5 * _L0_ffn_ref(_layernorm(x, axis=-1), L0_ffn_router_W, L0_ffn_router_b, L0_ffn_W1, L0_ffn_b1, L0_ffn_W2, L0_ffn_b2)
    x = x + _L0_attn_ref(_layernorm(x, axis=-1), L0_attn_ln1_g, L0_attn_ln1_b, L0_attn_wq, L0_attn_wk, L0_attn_wv, L0_attn_wo, L0_attn_ln2_g, L0_attn_ln2_b, L0_attn_w1, L0_attn_w2)
    x = x + 0.5 * _L0_ffn_ref(_layernorm(x, axis=-1), L0_ffn_router_W, L0_ffn_router_b, L0_ffn_W1, L0_ffn_b1, L0_ffn_W2, L0_ffn_b2)
    return x

_drawn_inputs = setup_inputs


def setup_inputs(seed=0):
    import zlib

    import numpy as np

    out = dict(_drawn_inputs(seed))
    spreads = {'L0_attn_ln1_g': (1.0, 0.6),
     'L0_attn_ln1_b': (0.0, 0.8),
     'L0_attn_ln2_g': (1.0, 0.6),
     'L0_attn_ln2_b': (0.0, 2.0),
     'L0_ffn_router_b': (0.0, 0.719),
     'L0_ffn_b1': (0.0, 0.8),
     'L0_ffn_b2': (0.0, 0.708)}
    factors = {'L0_attn_wq': 8.0,
     'L0_attn_wk': 8.0,
     'L0_attn_wv': 8.0,
     'L0_attn_wo': 8.0,
     'L0_ffn_router_W': 6.52,
     'L0_ffn_W1': 8.0,
     'L0_ffn_W2': 8.0}
    for name, (base, spread) in spreads.items():
        noise = np.random.default_rng([zlib.crc32(name.encode()), seed]).standard_normal(out[name].shape)
        drawn = base * np.exp(spread * noise) if base else spread * noise
        out[name] = jnp.asarray(drawn.astype(out[name].dtype))
    for name, factor in factors.items():
        out[name] = (out[name] * factor).astype(out[name].dtype)
    return out
```

```python
import numpy as np
import concourse.bass as bass
from concourse import mybir
from contextlib import ExitStack

P = 128
D = 128
B = 4
S = 512
TOK = B * S
T = TOK // P
GT = S // P
NG = T // GT
NE = 8
F = 512
FC = F // P
H = 16
DH = D // H
LEVELS = 256
HALF = LEVELS // 2
NT = (TOK + NE * (P - 1)) // P
RING = 4
EPS = 1e-5
MAGIC = 1.5 * 2.0 ** 23
QBASE = 2.0 ** 23
XB = FC + D


def bc(ap, shape):
    return ap.broadcast_to(list(shape))


def macaron_kernel(nc, x_d, g1_d, b1_d, wq_d, wk_d, wv_d, wo_d, g2_d, b2_d, w1_d, w2_d,
                   rw_d, rb_d, ew1_d, eb1_d, ew2_d, eb2_d, out_d):
    f32, bf16 = mybir.dt.float32, mybir.dt.bfloat16
    i16, i32, u32 = mybir.dt.int16, mybir.dt.int32, mybir.dt.uint32
    ALU, ACT, AX = mybir.AluOpType, mybir.ActivationFunctionType, mybir.AxisListType.X

    x_v = x_d.rearrange("b (t p) d -> p (b t) d", p=P)
    out_v = out_d.rearrange("b (t p) d -> p (b t) d", p=P)
    xn_scr = nc.dram_tensor("xn_scratch", [TOK, D], f32, kind="Internal").ap()
    y_scr = nc.dram_tensor("y_scratch", [NT * P, D], f32, kind="Internal").ap()
    xn_scr_v = xn_scr.rearrange("(t p) d -> p t d", p=P)
    y_scr_v = y_scr.rearrange("(t p) d -> t p d", p=P)

    ctx = ExitStack()
    with ctx:
        def sb(name, shape, dt=f32):
            return ctx.enter_context(nc.sbuf_tensor(name, shape, dt))

        def sem(name):
            return ctx.enter_context(nc.semaphore(name))

        x = sb("x", [P, T, D])
        xi = sb("xi", [P, T, D])
        xn = sb("xn", [P, T, D])
        stat = sb("stat", [P, GT, 6])
        mv = sb("mv", [P, T, 2])
        vin = sb("vin", [P, 2, GT, 2])
        rstd = sb("rstd", [P, T, 2])
        wq = sb("wq", [D, D])
        wkv = sb("wkv", [D, 2 * D])
        wo = sb("wo", [D, D])
        w1 = sb("w1", [D, F])
        w2 = sb("w2", [P, FC, D])
        rw = sb("rw", [D, NE])
        rb = sb("rb", [P, NE])
        gb = sb("gb", [D, 4])
        ew2 = sb("ew2", [P, NE, FC, D])
        eb1r = sb("eb1r", [NE * FC, P])
        ebias = sb("ebias", [P, NE, XB])
        ident = sb("ident", [P, P])
        ones_bf = sb("ones_bf", [P, P], bf16)
        before = sb("before", [P, P], bf16)
        bmask = sb("bmask", [P, H, DH])
        hmask = sb("hmask", [P, H])
        prefer = sb("prefer", [P, NE])
        ltE = sb("ltE", [P, NE, NE])
        rowid = sb("rowid", [P, P], bf16)
        tileid = sb("tileid", [P, NT])
        tokbase = sb("tokbase", [P, T], bf16)
        pcol = sb("pcol", [P, 1])
        mhalf = sb("mhalf", [P, GT, 2])
        xnT = sb("xnT", [D, T, P])
        lg = sb("lg", [P, T, NE])
        lmax = sb("lmax", [P, T])
        ex = sb("ex", [P, T, NE])
        key = sb("key", [P, T, NE])
        kmax = sb("kmax", [P, T])
        oh = sb("oh", [P, T, NE], bf16)
        psum_e = sb("psum_e", [P, T])
        gate = sb("gate", [P, T])
        ncnt = sb("ncnt", [P, NE])
        cnt = sb("cnt", [P, NE])
        cm = sb("cm", [P, NE, NE])
        sx = sb("sx", [P, NE])
        send = sb("send", [P, NE])
        ek_c = sb("ek_c", [P, NT, NE])
        eidf = sb("eidf", [P, NT])
        eid = sb("eid", [P, NT], i32)
        v3 = sb("v3", [P, T, NE])
        pos = sb("pos", [P, T])
        qf = sb("qf", [P, T])
        rf = sb("rf", [P, T])
        posu = sb("posu", [P, T], u32)
        inq = sb("inq", [P, T, NT], bf16)
        inqt = sb("inqt", [P, T, NT], bf16)
        inqp = sb("inqp", [P, T, NT], bf16)
        inr = sb("inr", [P, T, P], bf16)
        srcu = sb("srcu", [P, NT], u32)
        Xg = sb("Xg", [P, RING, D])
        W1c = sb("W1c", [D, RING, F])
        bb = sb("bb", [P, RING, XB])
        xT = sb("xT", [D, RING, P])
        hT = sb("hT", [P, RING, F])
        ysb = sb("ysb", [P, NT, D])
        Yg = sb("Yg", [P, T, D])
        h1 = sb("h1", [P, 2, GT, D])
        h1T = sb("h1T", [D, 2, S])
        eq = sb("eq", [D, 2, S])
        rq = sb("rq", [D, 2, S])
        phiq = sb("phiq", [D, 2, S])
        ek = sb("ek", [P, 2, GT, D])
        rk = sb("rk", [P, 2, GT, D])
        phik = sb("phik", [P, 2, GT, D])
        vx = sb("vx", [P, 2, GT, D + 1])
        zc = sb("zc", [P, 2])
        KVm = sb("KVm", [P, 2, D + H])
        den = sb("den", [P, 2, GT, H])
        rden = sb("rden", [P, 2, GT, H])
        att = sb("att", [P, 2, GT, D])
        attT = sb("attT", [D, 2, S])
        qa = sb("qa", [P, FC, S])
        qb = sb("qb", [P, FC, S])
        actT = sb("actT", [P, 2, FC, S])
        gelu_bias = sb("gelu_bias", [P, 1])

        bank = [ctx.enter_context(nc.psum_tensor(f"bank{i}", [P, 512], f32)) for i in range(8)]

        x_in = [sem(f"x_in{g}") for g in range(NG)]
        rw_in = sem("rw_in")
        eb_in = sem("eb_in")
        w_in = sem("w_in")
        ew2_in = sem("ew2_in")
        const_ready = sem("const_ready")
        pool_chain = sem("pool_chain")
        dve_chain = sem("dve_chain")
        ebias_ready = sem("ebias_ready")
        eb1_T = sem("eb1_T")
        stats_ready = sem("stats_ready")
        rstd_ready = sem("rstd_ready")
        xn_ready = sem("xn_ready")
        xn_stored = sem("xn_stored")
        xnT_ps = sem("xnT_ps")
        xnT_ready = sem("xnT_ready")
        logits_ps = sem("logits_ps")
        lg_ready = sem("lg_ready")
        ex_ready = sem("ex_ready")
        oh_ready = sem("oh_ready")
        rank_ps = sem("rank_ps")
        eid_ready = sem("eid_ready")
        pos_ready = sem("pos_ready")
        inq_ready = sem("inq_ready")
        inr_ready = sem("inr_ready")
        src_ps = sem("src_ps")
        src_ready = sem("src_ready")
        g_in = [sem(f"g_in{u}") for u in range(RING)]
        w1c_in = [sem(f"w1c_in{u}") for u in range(RING)]
        xg_T = sem("xg_T")
        xT_ready = sem("xT_ready")
        h_ps = sem("h_ps")
        hT_ready = sem("hT_ready")
        y_ps = sem("y_ps")
        y_ready = sem("y_ready")
        y_stored = sem("y_stored")
        yg_in = [sem(f"yg_in{g}") for g in range(NG)]
        h1_ready = sem("h1_ready")
        h1T_ps = sem("h1T_ps")
        h1T_ready = sem("h1T_ready")
        q_ps = sem("q_ps")
        kv_ps = sem("kv_ps")
        q_out = sem("q_out")
        kv_out = sem("kv_out")
        phiq_ready = sem("phiq_ready")
        phik_ready = sem("phik_ready")
        ones_ready = sem("ones_ready")
        kvsum_ps = sem("kvsum_ps")
        KVm_ready = sem("KVm_ready")
        num_ps = sem("num_ps")
        att_ready = sem("att_ready")
        attT_ps = sem("attT_ps")
        attT_ready = sem("attT_ready")
        wo_ps = sem("wo_ps")
        x2_ready = sem("x2_ready")
        h2_ready = sem("h2_ready")
        h2T_ps = sem("h2T_ps")
        h2T_ready = sem("h2T_ready")
        u_ps = sem("u_ps")
        qa_ready = sem("qa_ready")
        qb_ready = sem("qb_ready")
        act_ready = sem("act_ready")
        w2_ps = sem("w2_ps")
        x3_ready = sem("x3_ready")
        res_ready = sem("res_ready")
        out_ready = sem("out_ready")
        out_done = sem("out_done")

        LN = ([("m0", g) for g in range(NG)] + [("a", 0), ("a", 1)]
              + [k for b in range(B) for k in ([("a", b + 2)] if b + 2 < B else []) + [("l", b)]]
              + [("m1", g) for g in range(NG)])
        LN_AT = {k: i + 1 for i, k in enumerate(LN)}
        slots = [len(range(u, NT, RING)) for u in range(RING)]
        LOOPS = (NT - 3) // RING
        REST = range(LOOPS * RING, NT)

        class Tile:

            def __init__(self, i, n):
                self.slot, self.round = n % RING, i + n // RING
                self.k, self.parity = i * RING + n, n % 2

        def expert_tiles(eng, step):
            with eng.Fori(0, LOOPS) as i:
                for n in range(RING):
                    step(i, n)
            for k in REST:
                step(LOOPS, k - LOOPS * RING)

        def left(i, n):
            return not isinstance(i, int) or i * RING + n < NT

        block = ctx.enter_context(nc.Block())

        @block.sync
        def _(sp):
            for g in range(NG):
                sp.dma_start(x[:, g * GT:(g + 1) * GT, :], x_v[:, g * GT:(g + 1) * GT, :]).then_inc(x_in[g], 16)
            sp.dma_start(rw[:, :], rw_d).then_inc(rw_in, 16)
            sp.dma_start(rb[:, :], rb_d.unsqueeze(0).broadcast_to([P, NE])).then_inc(rw_in, 16)
            sp.dma_start(eb1r[:, :], eb1_d.rearrange("e (c p) -> (e c) p", p=P)).then_inc(eb_in, 16)
            sp.dma_start(ebias[:, :, FC:XB], eb2_d.unsqueeze(0).broadcast_to([P, NE, D])).then_inc(eb_in, 16)
            sp.dma_start(ew2[:, :, :, :], ew2_d.rearrange("e (c p) d -> p e c d", p=P)).then_inc(ew2_in, 16)
            for dst, src in ((wq[:, :], wq_d), (wkv[:, 0:D], wk_d), (wkv[:, D:2 * D], wv_d), (wo[:, :], wo_d),
                             (w1[:, :], w1_d), (w2[:, :, :], w2_d.rearrange("(c p) d -> p c d", p=P))):
                sp.dma_start(dst, src).then_inc(w_in, 16)
            for j, v in enumerate((g1_d, b1_d, g2_d, b2_d)):
                sp.dma_start(gb[:, j:j + 1], v.rearrange("(d a) -> d a", a=1)).then_inc(w_in, 16)
            for m in range(2):
                for g in range(NG):
                    sp.wait_ge(xn_ready, m * NG + g + 1)
                    sp.dma_start(xn_scr_v[:, g * GT:(g + 1) * GT, :],
                                 xn[:, g * GT:(g + 1) * GT, :]).then_inc(xn_stored, 16)
                sp.wait_ge(eid_ready, m + 1)
                sp.wait_ge(ebias_ready, 1)

                def load_expert(i, n):
                    t = Tile(i, n)
                    e = sp.value_load(eid[0:1, bass.ds(t.k, 1)], min_val=0, max_val=NE - 1)
                    sp.dma_start(W1c[:, t.slot, :], ew1_d[bass.ds(e, 1), :, :].squeeze(0)
                                 ).then_inc(w1c_in[t.slot], 16)
                    sp.dma_start(bb[:, t.slot, :], ebias[:, bass.ds(e, 1), :].squeeze(1)
                                 ).then_inc(w1c_in[t.slot], 16)

                for n in range(RING):
                    load_expert(0, n)

                def store_y(i, n):
                    t = Tile(i, n)
                    sp.wait_ge(y_ready, m * NT + 1 + t.k)
                    sp.dma_start(y_scr_v[bass.ds(t.k, 1), :, :].squeeze(0),
                                 ysb[:, bass.ds(t.k, 1), :].squeeze(1)).then_inc(y_stored, 16)

                def step(i, n):
                    store_y(i, n)
                    if left(i, n + RING):
                        load_expert(i, n + RING)

                with sp.Fori(0, LOOPS - 1) as i:
                    for n in range(RING):
                        step(i, n)
                for k in range((LOOPS - 1) * RING, NT):
                    step(LOOPS - 1, k - (LOOPS - 1) * RING)
            for g in range(NG):
                sp.wait_ge(out_ready, g + 1)
                sp.dma_start(out_v[:, g * GT:(g + 1) * GT, :], x[:, g * GT:(g + 1) * GT, :]).then_inc(out_done, 16)
            sp.wait_ge(out_done, 16 * NG)

        @block.gpsimd
        def _(pool):
            chain = [0]

            def link(ins):
                chain[0] += 1
                ins.then_inc(pool_chain, 1)
                pool.wait_ge(pool_chain, chain[0])

            g = nc.gpsimd
            g.memset(ident[:, :], 0.0).then_inc(pool_chain, 1)
            g.memset(ones_bf[:, :], 1.0).then_inc(pool_chain, 1)
            g.memset(bmask[:, :, :], 1.0).then_inc(pool_chain, 1)
            g.memset(hmask[:, :], 1.0).then_inc(pool_chain, 1)
            g.memset(ltE[:, :, :], 1.0).then_inc(pool_chain, 1)
            g.memset(before[:, :], 1.0).then_inc(pool_chain, 1)
            chain[0] += 6
            g.memset(mhalf[:, :, :], -0.5).then_inc(const_ready, 1)
            pool.wait_ge(pool_chain, chain[0])
            g.affine_select(out=ident[:, :], in_=ident[:, :], compare_op=ALU.not_equal, fill=1.0, base=0,
                            pattern=[[-1, P]], channel_multiplier=1).then_inc(const_ready, 1)

            def normaliser(at):
                kind, n = LN[at]
                pool.wait_ge(stats_ready, at + 1)
                a = at % 2
                v = mv[:, n * GT:(n + 1) * GT, 1:2]
                g.tensor_scalar(vin[:, a, :, 0:1], v, 1.0, EPS, ALU.mult, ALU.add).then_inc(pool_chain, 1)
                g.tensor_scalar(vin[:, a, :, 1:2], v, 1.0 + EPS, EPS * EPS, ALU.mult, ALU.add).then_inc(pool_chain, 1)
                chain[0] += 2
                pool.wait_ge(pool_chain, chain[0])
                wide = 2 if kind == "a" else 1
                g.tensor_tensor(out=rstd[:, n * GT:(n + 1) * GT, 0:wide], in0=vin[:, a, :, 0:wide],
                                in1=mhalf[:, :, 0:wide], op=ALU.pow).then_inc(rstd_ready, 1)

            pool.wait_ge(const_ready, 2)
            for at in range(NG):
                normaliser(at)
            g.affine_select(out=before[:, :], in_=before[:, :], compare_op=ALU.is_gt, fill=0.0, base=0,
                            pattern=[[1, P]], channel_multiplier=-1).then_inc(const_ready, 1)
            g.affine_select(out=ltE[:, :, :], in_=ltE[:, :, :], compare_op=ALU.is_gt, fill=0.0, base=0,
                            pattern=[[1, NE], [-1, NE]], channel_multiplier=0).then_inc(const_ready, 1)
            g.iota(prefer[:, :], [[-1, NE]], base=NE, channel_multiplier=0,
                   allow_small_or_imprecise_dtypes=True).then_inc(const_ready, 1)
            g.iota(rowid[:, :], [[1, P]], base=0, channel_multiplier=0,
                   allow_small_or_imprecise_dtypes=True).then_inc(const_ready, 1)
            g.iota(tileid[:, :], [[1, NT]], base=0, channel_multiplier=0,
                   allow_small_or_imprecise_dtypes=True).then_inc(const_ready, 1)
            g.iota(tokbase[:, :], [[P, T]], base=0, channel_multiplier=0,
                   allow_small_or_imprecise_dtypes=True).then_inc(const_ready, 1)
            g.iota(pcol[:, :], [[0, 1]], base=0, channel_multiplier=1,
                   allow_small_or_imprecise_dtypes=True).then_inc(const_ready, 1)
            for m_, pat in ((bmask[:, :, :], [[-DH, H], [0, DH]]), (hmask[:, :], [[-DH, H]])):
                link(g.affine_select(out=m_, in_=m_, compare_op=ALU.is_ge, fill=0.0, base=0,
                                     pattern=pat, channel_multiplier=1))
                g.affine_select(out=m_, in_=m_, compare_op=ALU.is_ge, fill=0.0, base=DH - 1,
                                pattern=[[-s_, n_] for s_, n_ in pat], channel_multiplier=-1).then_inc(const_ready, 1)
            g.memset(gelu_bias[:, :], -0.1 * HALF).then_inc(const_ready, 1)
            g.memset(vx[:, :, :, D:D + 1], 1.0).then_inc(ones_ready, 1)

            def gather_tokens(m):
                pool.wait_ge(xn_stored, 16 * NG * (m + 1))
                pool.wait_ge(src_ready, m + 1)
                for k in range(NT):
                    if k >= RING:
                        pool.wait_ge(xg_T, m * NT + k - RING + 1)
                    g.indirect_dma_start(out=Xg[:, k % RING, :], out_offset=None, in_=xn_scr,
                                         in_offset=bass.IndirectOffsetOnAxis(ap=srcu[:, k:k + 1], axis=0)
                                         ).then_inc(g_in[k % RING], 16)

            def gather_results(m):
                pool.wait_ge(y_stored, 16 * NT * (m + 1))
                for t in range(T):
                    g.indirect_dma_start(out=Yg[:, t, :], out_offset=None, in_=y_scr,
                                         in_offset=bass.IndirectOffsetOnAxis(ap=posu[:, t:t + 1], axis=0)
                                         ).then_inc(yg_in[t // GT], 16)

            gather_tokens(0)
            gather_results(0)
            for at in range(NG, NG + 2 * B):
                normaliser(at)
            for b in range(B):
                pool.wait_ge(h2_ready, b + 1)
                g.tensor_tensor(out=xi[:, b * GT:(b + 1) * GT, :], in0=xi[:, b * GT:(b + 1) * GT, :],
                                in1=x[:, b * GT:(b + 1) * GT, :], op=ALU.add).then_inc(res_ready, 1)
            for at in range(NG + 2 * B, len(LN)):
                normaliser(at)
            gather_tokens(1)
            gather_results(1)

        @block.scalar
        def _(act):
            A = nc.scalar.activation

            def front(m):
                for g in range(NG):
                    act.wait_ge(xnT_ps, m * NG + g + 1)
                    A(xnT[:, g * GT:(g + 1) * GT, :], bank[g % 2][:, :], ACT.Copy).then_inc(xnT_ready, 1)
                act.wait_ge(lg_ready, m + 1)
                A(ex[:, :, :], lg[:, :, :], ACT.Exp).then_inc(ex_ready, 1)

            def experts(m):
                def step(i, n):
                    t = Tile(i, n)
                    act.wait_ge(h_ps, m * NT + 1 + t.k)
                    for c in range(FC):
                        last = A(hT[:, t.slot, c * P:(c + 1) * P], bank[2 + t.parity][:, c * P:(c + 1) * P],
                                 ACT.Relu, bias=bb[:, t.slot, c:c + 1])
                    last.then_inc(hT_ready, 1)
                expert_tiles(act, step)

            front(0)
            experts(0)
            act.wait_ge(w_in, 16 * 10)
            act.wait_ge(ones_ready, 1)

            def project_out(b):
                s = b % 2
                act.wait_ge(h1T_ps, b + 1)
                A(h1T[:, s, :], bank[0][:, :], ACT.Identity, scale=gb[:, 0:1], bias=gb[:, 1:2]).then_inc(h1T_ready, 1)
                act.wait_ge(q_ps, b + 1)
                A(eq[:, s, :], bank[2][:, :], ACT.Exp)
                A(rq[:, s, :], bank[2][:, :], ACT.Relu).then_inc(q_out, 1)
                act.wait_ge(kv_ps, b + 1)
                for j in range(2):
                    kv = bank[3 + j][:, :].rearrange("p (t n) -> p t n", t=2)
                    A(ek[:, s, 2 * j:2 * j + 2, :], kv[:, :, 0:D], ACT.Exp)
                    A(rk[:, s, 2 * j:2 * j + 2, :], kv[:, :, 0:D], ACT.Relu)
                    A(vx[:, s, 2 * j:2 * j + 2, 0:D], kv[:, :, D:2 * D], ACT.Copy).then_inc(kv_out, 1)

            project_out(0)
            for b in range(B):
                if b + 1 < B:
                    project_out(b + 1)
                act.wait_ge(attT_ps, b + 1)
                A(attT[:, b % 2, :], bank[1][:, :], ACT.Copy).then_inc(attT_ready, 1)

            def norm2(b):
                act.wait_ge(h2T_ps, b + 1)
                A(h1T[:, b % 2, :], bank[b % 2][:, :], ACT.Identity, scale=gb[:, 2:3], bias=gb[:, 3:4]
                  ).then_inc(h2T_ready, 1)

            norm2(0)
            for b in range(B):
                if b + 1 < B:
                    norm2(b + 1)
                for c in range(FC):
                    act.wait_ge(qb_ready, b * FC + c + 1)
                    level = qb[:, c, :].bitcast(i16).rearrange("p (n two) -> p n two", two=2)[:, :, 0]
                    A(actT[:, b % 2, c, :], level, ACT.Gelu_apprx_tanh, scale=0.1,
                      bias=gelu_bias[:, 0:1]).then_inc(act_ready, 1)
            front(1)
            experts(1)

        @block.tensor
        def _(pe):
            mm = nc.tensor.matmul

            pe.wait_ge(eb_in, 32)
            pe.wait_ge(const_ready, 2)
            nc.tensor.transpose(bank[5][:, 0:NE * FC], eb1r[:, :], ident[0:NE * FC, 0:NE * FC]).then_inc(eb1_T, 1)
            pe.wait_ge(rw_in, 32)

            def front(m):
                def transposes(g):
                    pe.wait_ge(xn_ready, m * NG + g + 1)
                    if g >= 2:
                        pe.wait_ge(xnT_ready, m * NG + g - 1)
                    for j in range(GT):
                        last = nc.tensor.transpose(bank[g % 2][:, j * P:(j + 1) * P], xn[:, g * GT + j, :], ident[:, :])
                    last.then_inc(xnT_ps, 1)

                transposes(0)
                for g in range(NG):
                    if g + 1 < NG:
                        transposes(g + 1)
                    pe.wait_ge(xnT_ready, m * NG + g + 1)
                    for t in range(g * GT, (g + 1) * GT):
                        last = mm(bank[2][:, t * NE:(t + 1) * NE], xnT[:, t, :], rw[:, :], start=True, stop=True)
                last.then_inc(logits_ps, 1)

            def ranks(m):
                R = bank[3]
                pe.wait_ge(oh_ready, m + 1)
                pe.wait_ge(const_ready, 12)

                def spread(t):
                    n = T - t
                    return bc(oh[:, t, :].unsqueeze(1), [P, n, NE])

                mm(R[:, NE:(T + 1) * NE], ones_bf[:, :], spread(0), start=True, stop=False, skip_group_check=True)
                mm(R[:, 0:NE], before[:, :], oh[:, 0, :], start=False, stop=False, skip_group_check=True)
                mm(R[:, NE:T * NE], before[:, :], oh[:, 1:T, :], start=False, stop=False, skip_group_check=True)
                for t in range(1, T):
                    last = mm(R[:, (t + 1) * NE:(T + 1) * NE], ones_bf[:, :], spread(t),
                              start=False, stop=t == T - 1, skip_group_check=True)
                last.then_inc(rank_ps, 1)

            def sources(m):
                pe.wait_ge(inq_ready, m + 1)
                for t in range(T):
                    pe.wait_ge(inr_ready, m * T + t + 1)
                    mm(bank[4][:, 0:NT], inr[:, t, :], inqt[:, t, :], start=t == 0, stop=False)
                    last = mm(bank[4][:, 0:NT], inr[:, t, :], inqp[:, t, :], start=False, stop=t == T - 1)
                last.then_inc(src_ps, 1)

            def experts(m):
                pe.wait_ge(eid_ready, m + 1)
                pe.wait_ge(ew2_in, 16)

                def turn(i, n):
                    t = Tile(i, n)
                    pe.wait_ge(g_in[t.slot], 16 * (m * slots[t.slot] + 1 + t.round))
                    nc.tensor.transpose(bank[t.parity][:, 0:P], Xg[:, t.slot, :], ident[:, :]).then_inc(xg_T, 1)

                def up(i, n):
                    t = Tile(i, n)
                    pe.wait_ge(w1c_in[t.slot], 32 * (m * slots[t.slot] + 1 + t.round))
                    pe.wait_ge(xT_ready, m * NT + 1 + t.k)
                    for c in range(FC):
                        last = mm(bank[2 + t.parity][:, c * P:(c + 1) * P], W1c[:, t.slot, c * P:(c + 1) * P],
                                  xT[:, t.slot, :], start=True, stop=True)
                    last.then_inc(h_ps, 1)

                def down(i, n):
                    t = Tile(i, n)
                    e = pe.value_load(eid[0:1, bass.ds(t.k, 1)], min_val=0, max_val=NE - 1)
                    pe.wait_ge(hT_ready, m * NT + 1 + t.k)
                    if not left(i, n + 1):
                        pe.wait_ge(y_ready, m * NT + t.k - 1)
                    for c in range(FC):
                        last = mm(bank[4 + t.parity][:, 0:D], hT[:, t.slot, c * P:(c + 1) * P],
                                  ew2[:, bass.ds(e, 1), c, :].squeeze(1), start=c == 0, stop=c == FC - 1)
                    last.then_inc(y_ps, 1)

                turn(0, 0)
                turn(0, 1)
                up(0, 0)

                def step(i, n):
                    if left(i, n + 2):
                        turn(i, n + 2)
                    if left(i, n + 1):
                        up(i, n + 1)
                    down(i, n)
                expert_tiles(pe, step)

            front(0)
            ranks(0)
            sources(0)
            experts(0)
            pe.wait_ge(w_in, 16 * 10)

            def project(b):
                s = b % 2
                pe.wait_ge(h1_ready, b + 1)
                for j in range(GT):
                    last = nc.tensor.transpose(bank[0][:, j * P:(j + 1) * P], h1[:, s, j, :], ident[:, :])
                last.then_inc(h1T_ps, 1)
                pe.wait_ge(h1T_ready, b + 1)
                if b >= 1:
                    pe.wait_ge(q_out, b)
                mm(bank[2][:, :], wq[:, :], h1T[:, s, :], start=True, stop=True).then_inc(q_ps, 1)
                if b >= 1:
                    pe.wait_ge(kv_out, 2 * b)
                for j in range(GT):
                    last = mm(bank[3 + j // 2][:, (j % 2) * 2 * D:(j % 2 + 1) * 2 * D],
                              h1T[:, s, j * P:(j + 1) * P], wkv[:, :], start=True, stop=True)
                last.then_inc(kv_ps, 1)

            def attend(b):
                s = b % 2
                pe.wait_ge(phik_ready, b + 1)
                if b >= 1:
                    pe.wait_ge(x2_ready, b)
                for j in range(GT):
                    last = mm(bank[5][:, 0:D + 1], phik[:, s, j, :], vx[:, s, j, :], start=j == 0, stop=j == GT - 1)
                last.then_inc(kvsum_ps, 1)
                pe.wait_ge(KVm_ready, b + 1)
                pe.wait_ge(phiq_ready, b + 1)
                for j in range(GT):
                    last = mm(bank[6 + j // 2][:, (j % 2) * (D + H):(j % 2 + 1) * (D + H)],
                              phiq[:, s, j * P:(j + 1) * P], KVm[:, s, :], start=True, stop=True)
                last.then_inc(num_ps, 1)
                pe.wait_ge(att_ready, b + 1)
                for j in range(GT):
                    last = nc.tensor.transpose(bank[1][:, j * P:(j + 1) * P], att[:, s, j, :], ident[:, :])
                last.then_inc(attT_ps, 1)
                pe.wait_ge(attT_ready, b + 1)
                for j in range(GT):
                    last = mm(bank[5][:, j * P:(j + 1) * P], attT[:, s, j * P:(j + 1) * P], wo[:, :],
                              start=True, stop=True)
                last.then_inc(wo_ps, 1)

            project(0)
            for b in range(B):
                if b + 1 < B:
                    project(b + 1)
                attend(b)

            def turn2(b):
                pe.wait_ge(h2_ready, b + 1)
                if b >= 2:
                    pe.wait_ge(h2T_ready, b - 1)
                for j in range(GT):
                    last = nc.tensor.transpose(bank[b % 2][:, j * P:(j + 1) * P], h1[:, b % 2, j, :], ident[:, :])
                last.then_inc(h2T_ps, 1)

            def up2(b):
                pe.wait_ge(h2T_ready, b + 1)
                for c in range(FC):
                    if b >= 1:
                        pe.wait_ge(qa_ready, (b - 1) * FC + c + 1)
                    mm(bank[2 + c][:, :], w1[:, c * P:(c + 1) * P], h1T[:, b % 2, :], start=True, stop=True
                       ).then_inc(u_ps, 1)

            turn2(0)
            up2(0)
            for b in range(B):
                if b + 1 < B:
                    turn2(b + 1)
                    up2(b + 1)
                if b >= 2:
                    pe.wait_ge(x3_ready, b - 1)
                pe.wait_ge(act_ready, (b + 1) * FC)
                for j in range(GT):
                    for c in range(FC):
                        last = mm(bank[6 + b % 2][:, j * P:(j + 1) * P], actT[:, b % 2, c, j * P:(j + 1) * P],
                                  w2[:, c, :], start=c == 0, stop=c == FC - 1)
                last.then_inc(w2_ps, 1)
            front(1)
            ranks(1)
            sources(1)
            experts(1)

        @block.vector
        def _(dve):
            chain = [0]
            v = nc.vector

            def link(ins):
                chain[0] += 1
                ins.then_inc(dve_chain, 1)
                dve.wait_ge(dve_chain, chain[0])

            def statistics(kind, n, src):
                for j in range(GT):
                    last = v.bn_stats(stat[:, j, :], src[:, n * GT + j, :])
                link(last)
                for j in range(GT):
                    last = v.bn_aggr(mv[:, n * GT + j, :], stat[:, j, :])
                last.then_inc(stats_ready, 1)
                dve.wait_ge(stats_ready, LN_AT[kind, n])

            def normalise(dst, src, n, which=0):
                for j in range(GT):
                    t = n * GT + j
                    last = v.tensor_scalar(dst(j), src[:, t, :], mv[:, t, 0:1], rstd[:, t, which:which + 1],
                                           ALU.subtract, ALU.mult)
                return last

            def route(m):
                dve.wait_ge(logits_ps, m + 1)
                link(v.tensor_tensor(out=lg[:, :, :], in0=bank[2][:, 0:T * NE].rearrange("p (t e) -> p t e", e=NE),
                                     in1=bc(rb[:, :].unsqueeze(1), [P, T, NE]), op=ALU.add))
                link(v.tensor_reduce(lmax[:, :], lg[:, :, :], AX, ALU.max))
                v.tensor_tensor(out=lg[:, :, :], in0=lg[:, :, :], in1=bc(lmax[:, :].unsqueeze(2), [P, T, NE]),
                                op=ALU.subtract).then_inc(lg_ready, 1)
                dve.wait_ge(lg_ready, m + 1)
                if m == 0:
                    dve.wait_ge(const_ready, 12)
                link(v.scalar_tensor_tensor(out=key[:, :, :], in0=lg[:, :, :], scalar=0.0,
                                            in1=bc(prefer[:, :].unsqueeze(1), [P, T, NE]),
                                            op0=ALU.is_ge, op1=ALU.mult))
                link(v.tensor_reduce(kmax[:, :], key[:, :, :], AX, ALU.max))
                v.tensor_tensor(out=oh[:, :, :], in0=key[:, :, :], in1=bc(kmax[:, :].unsqueeze(2), [P, T, NE]),
                                op=ALU.is_equal).then_inc(oh_ready, 1)
                dve.wait_ge(oh_ready, m + 1)
                dve.wait_ge(ex_ready, m + 1)
                link(v.tensor_reduce(psum_e[:, :], ex[:, :, :], AX, ALU.add))
                link(v.reciprocal(gate[:, :], psum_e[:, :]))
                link(v.tensor_scalar(gate[:, :], gate[:, :], 0.5, None, ALU.mult))
                dve.wait_ge(rank_ps, m + 1)
                R = bank[3]
                link(v.tensor_scalar(ncnt[:, :], R[:, T * NE:(T + 1) * NE], 1.0 / P, (P - 1.0) / P - 0.498046875,
                                     ALU.mult, ALU.add))
                link(v.tensor_scalar(cnt[:, :], ncnt[:, :], MAGIC, MAGIC, ALU.add, ALU.subtract))
                link(v.tensor_tensor(out=cm[:, :, :], in0=bc(cnt[:, :].unsqueeze(1), [P, NE, NE]), in1=ltE[:, :, :],
                                     op=ALU.mult))
                link(v.tensor_reduce(sx[:, :], cm[:, :, :], AX, ALU.add))
                link(v.tensor_tensor(out=send[:, :], in0=sx[:, :], in1=cnt[:, :], op=ALU.add))
                link(v.tensor_tensor(out=ek_c[:, :, :], in0=bc(tileid[:, :].unsqueeze(2), [P, NT, NE]),
                                     in1=bc(send[:, :].unsqueeze(1), [P, NT, NE]), op=ALU.is_ge))
                link(v.tensor_reduce(eidf[:, :], ek_c[:, :, :], AX, ALU.add))
                v.tensor_scalar(eid[:, :], eidf[:, :], NE - 1.0, None, ALU.min).then_inc(eid_ready, 1)
                link(v.scalar_tensor_tensor(out=v3[:, :, :], in0=bc(sx[:, :].unsqueeze(1), [P, T, NE]), scalar=float(P),
                                            in1=R[:, 0:T * NE].rearrange("p (t e) -> p t e", e=NE),
                                            op0=ALU.mult, op1=ALU.add))
                link(v.tensor_tensor(out=v3[:, :, :], in0=v3[:, :, :], in1=oh[:, :, :], op=ALU.mult))
                link(v.tensor_reduce(pos[:, :], v3[:, :, :], AX, ALU.add))
                link(v.tensor_scalar(qf[:, :], pos[:, :], 1.0 / P, -0.498046875, ALU.mult, ALU.add))
                link(v.tensor_scalar(qf[:, :], qf[:, :], MAGIC, MAGIC, ALU.add, ALU.subtract))
                link(v.scalar_tensor_tensor(out=rf[:, :], in0=qf[:, :], scalar=-float(P), in1=pos[:, :],
                                            op0=ALU.mult, op1=ALU.add))
                link(v.tensor_tensor(out=inq[:, :, :], in0=bc(tileid[:, :].unsqueeze(1), [P, T, NT]),
                                     in1=bc(qf[:, :].unsqueeze(2), [P, T, NT]), op=ALU.is_equal))
                v.tensor_tensor(out=inqt[:, :, :], in0=inq[:, :, :], in1=bc(tokbase[:, :].unsqueeze(2), [P, T, NT]),
                                op=ALU.mult)
                v.tensor_scalar(inqp[:, :, :], inq[:, :, :], pcol[:, 0:1], None, ALU.mult).then_inc(inq_ready, 1)
                for t in range(T):
                    v.tensor_scalar(inr[:, t, :], rowid[:, :], rf[:, t:t + 1], None, ALU.is_equal).then_inc(inr_ready, 1)
                v.tensor_copy(posu[:, :], pos[:, :]).then_inc(pos_ready, 1)
                dve.wait_ge(src_ps, m + 1)
                v.tensor_copy(srcu[:, :], bank[4][:, 0:NT]).then_inc(src_ready, 1)

            def experts(m):
                def take_x(i, n):
                    t = Tile(i, n)
                    dve.wait_ge(xg_T, m * NT + 1 + t.k)
                    v.tensor_copy(xT[:, t.slot, :], bank[t.parity][:, 0:P]).then_inc(xT_ready, 1)

                def take_y(i, n):
                    t = Tile(i, n)
                    dve.wait_ge(y_ps, m * NT + 1 + t.k)
                    v.tensor_tensor(out=ysb[:, bass.ds(t.k, 1), :].squeeze(1), in0=bank[4 + t.parity][:, 0:D],
                                    in1=bb[:, t.slot, FC:XB], op=ALU.add).then_inc(y_ready, 1)

                take_x(0, 0)
                take_x(0, 1)

                def step(i, n):
                    if left(i, n + 2):
                        take_x(i, n + 2)
                    take_y(i, n)
                expert_tiles(dve, step)

            def combine(m, g):
                dve.wait_ge(yg_in[g], 16 * GT * (m + 1))
                for t in range(g * GT, (g + 1) * GT):
                    last = v.scalar_tensor_tensor(out=x[:, t, :], in0=Yg[:, t, :], scalar=gate[:, t:t + 1],
                                                  in1=x[:, t, :], op0=ALU.mult, op1=ALU.add)
                return last

            for g in range(NG):
                dve.wait_ge(x_in[g], 16)
                statistics("m0", g, x)
            for g in range(NG):
                dve.wait_ge(rstd_ready, LN_AT["m0", g])
                normalise(lambda j: xn[:, g * GT + j, :], x, g).then_inc(xn_ready, 1)
            dve.wait_ge(eb1_T, 1)
            v.tensor_copy(ebias[:, :, 0:FC], bank[5][:, 0:NE * FC].rearrange("p (e c) -> p e c", c=FC)
                          ).then_inc(ebias_ready, 1)
            route(0)
            experts(0)

            def begin(b):
                link(combine(0, b))
                statistics("a", b, x)

            def norm1(b):
                dve.wait_ge(rstd_ready, LN_AT["a", b])
                normalise(lambda j: xi[:, b * GT + j, :], x, b)
                normalise(lambda j: h1[:, b % 2, j, :], x, b, 1).then_inc(h1_ready, 1)

            def attend(b):
                s = b % 2
                dve.wait_ge(q_out, b + 1)
                v.scalar_tensor_tensor(out=phiq[:, s, :], in0=eq[:, s, :], scalar=1.0, in1=rq[:, s, :],
                                       op0=ALU.min, op1=ALU.add).then_inc(phiq_ready, 1)
                dve.wait_ge(kv_out, 2 * b + 2)
                v.scalar_tensor_tensor(out=phik[:, s, :, :], in0=ek[:, s, :, :], scalar=1.0, in1=rk[:, s, :, :],
                                       op0=ALU.min, op1=ALU.add).then_inc(phik_ready, 1)
                dve.wait_ge(kvsum_ps, b + 1)
                v.tensor_tensor(out=KVm[:, s, 0:D], in0=bank[5][:, 0:D], in1=bmask[:, :, :].rearrange("p h e -> p (h e)"),
                                op=ALU.mult)
                link(v.tensor_copy(zc[:, s:s + 1], bank[5][:, D:D + 1]))
                v.tensor_scalar(KVm[:, s, D:D + H], hmask[:, :], zc[:, s:s + 1], None, ALU.mult).then_inc(KVm_ready, 1)
                dve.wait_ge(num_ps, b + 1)
                nd = [bank[6 + j][:, 0:2 * (D + H)].rearrange("p (t n) -> p t n", t=2) for j in range(2)]
                for j in range(2):
                    last = v.tensor_scalar(den[:, s, 2 * j:2 * j + 2, :], nd[j][:, :, D:D + H], 1e-6, None, ALU.add)
                link(last)
                link(v.reciprocal(rden[:, s, :, :], den[:, s, :, :]))
                for t in range(GT):
                    last = v.tensor_tensor(
                        out=att[:, s, t, :].rearrange("p (h e) -> p h e", e=DH),
                        in0=nd[t // 2][:, t % 2, 0:D].rearrange("p (h e) -> p h e", e=DH),
                        in1=bc(rden[:, s, t, :].unsqueeze(2), [P, H, DH]), op=ALU.mult)
                last.then_inc(att_ready, 1)
                dve.wait_ge(wo_ps, b + 1)
                xb = xi[:, b * GT:(b + 1) * GT, :]
                v.tensor_tensor(out=xb, in0=bank[5][:, :].rearrange("p (t d) -> p t d", d=D), in1=xb, op=ALU.add
                                ).then_inc(x2_ready, 1)
                dve.wait_ge(x2_ready, b + 1)
                statistics("l", b, xi)

            begin(0)
            begin(1)
            norm1(0)
            for b in range(B):
                if b + 2 < B:
                    begin(b + 2)
                if b + 1 < B:
                    norm1(b + 1)
                attend(b)

            def norm2(b):
                dve.wait_ge(rstd_ready, LN_AT["l", b])
                normalise(lambda j: h1[:, b % 2, j, :], xi, b).then_inc(h2_ready, 1)

            norm2(0)
            for b in range(B):
                if b + 1 < B:
                    norm2(b + 1)
                for c in range(FC):
                    dve.wait_ge(u_ps, b * FC + c + 1)
                    v.tensor_scalar(qa[:, c, :], bank[2 + c][:, :], 10.0, QBASE + HALF, ALU.mult, ALU.add
                                    ).then_inc(qa_ready, 1)
                    dve.wait_ge(qa_ready, b * FC + c + 1)
                    if b >= 1:
                        dve.wait_ge(act_ready, (b - 1) * FC + c + 1)
                    v.tensor_scalar(qb[:, c, :], qa[:, c, :], QBASE, QBASE + LEVELS - 1, ALU.max, ALU.min
                                    ).then_inc(qb_ready, 1)
                dve.wait_ge(w2_ps, b + 1)
                dve.wait_ge(res_ready, b + 1)
                v.tensor_tensor(out=x[:, b * GT:(b + 1) * GT, :],
                                in0=bank[6 + b % 2][:, :].rearrange("p (t d) -> p t d", d=D),
                                in1=xi[:, b * GT:(b + 1) * GT, :], op=ALU.add).then_inc(x3_ready, 1)
                dve.wait_ge(x3_ready, b + 1)
                statistics("m1", b, x)

            for g in range(NG):
                dve.wait_ge(rstd_ready, LN_AT["m1", g])
                normalise(lambda j: xn[:, g * GT + j, :], x, g).then_inc(xn_ready, 1)
            route(1)
            experts(1)
            for g in range(NG):
                combine(1, g).then_inc(out_ready, 1)


_INS = ['L0_attn_x', 'L0_attn_ln1_g', 'L0_attn_ln1_b', 'L0_attn_wq', 'L0_attn_wk', 'L0_attn_wv', 'L0_attn_wo',
        'L0_attn_ln2_g', 'L0_attn_ln2_b', 'L0_attn_w1', 'L0_attn_w2', 'L0_ffn_router_W', 'L0_ffn_router_b',
        'L0_ffn_W1', 'L0_ffn_b1', 'L0_ffn_W2', 'L0_ffn_b2']
_OUTS = [((B, S, D), 'float32')]


def kernel(**inputs):
    import numpy as _np
    import concourse.bacc as _bacc
    from concourse import mybir as _mybir
    from concourse.bass_utils import run_bass_kernel_spmd as _run

    nc = _bacc.Bacc("TRN2", target_bir_lowering=False, num_devices=1)
    arrays, args = {}, []
    for name in _INS:
        a = _np.ascontiguousarray(inputs[name])
        arrays[f"in_{name}_dram"] = a
        args.append(nc.dram_tensor(f"in_{name}_dram", a.shape, _mybir.dt.from_np(a.dtype), kind="ExternalInput").ap())
    for i, (shape, dtype) in enumerate(_OUTS):
        dt = _mybir.dt.from_np(_np.dtype(dtype))
        args.append(nc.dram_tensor(f"out_{i}_dram", shape, dt, kind="ExternalOutput").ap())
    macaron_kernel(nc, *args)
    r = _run(nc, [arrays], core_ids=[0])
    got = tuple(r.results[0][f"out_{i}_dram"] for i in range(len(_OUTS)))
    return got[0]
```

```python
import numpy as np
import concourse.bass as bass
from concourse import mybir
from contextlib import ExitStack

P = 128
D = 128
B = 4
S = 512
TOK = B * S
T = TOK // P
GT = S // P
NG = T // GT
NE = 8
F = 512
FC = F // P
H = 16
DH = D // H
LEVELS = 256
HALF = LEVELS // 2
NT = (TOK + NE * (P - 1)) // P
RING = 4
EPS = 1e-5
MAGIC = 1.5 * 2.0 ** 23
QBASE = 2.0 ** 23
W1_AT, W2_AT, B1_AT, B2_AT, EW = 0, F, F + FC * D, F + FC * D + FC, F + FC * D + FC + D


def bc(ap, shape):
    return ap.broadcast_to(list(shape))


def macaron_kernel(nc, x_d, g1_d, b1_d, wq_d, wk_d, wv_d, wo_d, g2_d, b2_d, w1_d, w2_d,
                   rw_d, rb_d, ew1_d, eb1_d, ew2_d, eb2_d, out_d):
    f32, bf16 = mybir.dt.float32, mybir.dt.bfloat16
    i16, i32, u32 = mybir.dt.int16, mybir.dt.int32, mybir.dt.uint32
    ALU, ACT, AX = mybir.AluOpType, mybir.ActivationFunctionType, mybir.AxisListType.X

    x_v = x_d.rearrange("b (t p) d -> p (b t) d", p=P)
    out_v = out_d.rearrange("b (t p) d -> p (b t) d", p=P)
    xn_scr = nc.dram_tensor("xn_scratch", [TOK, D], f32, kind="Internal").ap()
    y_scr = nc.dram_tensor("y_scratch", [NT * P, D], f32, kind="Internal").ap()
    xn_scr_v = xn_scr.rearrange("(t p) d -> p t d", p=P)
    y_scr_v = y_scr.rearrange("(t p) d -> t p d", p=P)

    ctx = ExitStack()
    with ctx:
        def sb(name, shape, dt=f32):
            return ctx.enter_context(nc.sbuf_tensor(name, shape, dt))

        def sem(name):
            return ctx.enter_context(nc.semaphore(name))

        x = sb("x", [P, T, D])
        xi = sb("xi", [P, T, D])
        xn = sb("xn", [P, T, D])
        stat = sb("stat", [P, GT, 6])
        mv = sb("mv", [P, T, 2])
        vin = sb("vin", [P, 2, GT, 2])
        rstd = sb("rstd", [P, T, 2])
        wq = sb("wq", [D, D])
        wkv = sb("wkv", [D, 2 * D])
        wo = sb("wo", [D, D])
        w1 = sb("w1", [D, F])
        w2 = sb("w2", [P, FC, D])
        rw = sb("rw", [D, NE])
        rb = sb("rb", [P, NE])
        gb = sb("gb", [D, 4])
        eb1r = sb("eb1r", [NE * FC, P])
        ew = sb("ew", [P, NE, EW])
        ident = sb("ident", [P, P])
        ones_bf = sb("ones_bf", [P, P], bf16)
        before = sb("before", [P, P], bf16)
        bmask = sb("bmask", [P, H, DH])
        hmask = sb("hmask", [P, H])
        prefer = sb("prefer", [P, NE])
        ltE = sb("ltE", [P, NE, NE])
        rowid = sb("rowid", [P, P], bf16)
        tileid = sb("tileid", [P, NT])
        tokbase = sb("tokbase", [P, T], bf16)
        pcol = sb("pcol", [P, 1])
        mhalf = sb("mhalf", [P, GT, 2])
        xnT = sb("xnT", [D, T, P])
        lg = sb("lg", [P, T, NE])
        lmax = sb("lmax", [P, T])
        ex = sb("ex", [P, T, NE])
        key = sb("key", [P, T, NE])
        kmax = sb("kmax", [P, T])
        oh = sb("oh", [P, T, NE], bf16)
        psum_e = sb("psum_e", [P, T])
        gate = sb("gate", [P, T])
        ncnt = sb("ncnt", [P, NE])
        cnt = sb("cnt", [P, NE])
        cm = sb("cm", [P, NE, NE])
        sx = sb("sx", [P, NE])
        send = sb("send", [P, NE])
        ek_c = sb("ek_c", [P, NT, NE])
        eidf = sb("eidf", [P, NT])
        eid = sb("eid", [P, NT], i32)
        v3 = sb("v3", [P, T, NE])
        pos = sb("pos", [P, T])
        qf = sb("qf", [P, T])
        rf = sb("rf", [P, T])
        posu = sb("posu", [P, T], u32)
        inq = sb("inq", [P, T, NT], bf16)
        inqt = sb("inqt", [P, T, NT], bf16)
        inqp = sb("inqp", [P, T, NT], bf16)
        inr = sb("inr", [P, T, P], bf16)
        srcu = sb("srcu", [P, NT], u32)
        Xg = sb("Xg", [P, RING, D])
        ewc = sb("ewc", [P, RING, EW])
        xT = sb("xT", [D, RING, P])
        hT = sb("hT", [P, RING, F])
        ysb = sb("ysb", [P, NT, D])
        Yg = xnT
        h1 = sb("h1", [P, 2, GT, D])
        h1T = sb("h1T", [D, 2, S])
        eq = sb("eq", [D, 2, S])
        rq = sb("rq", [D, 2, S])
        phiq = sb("phiq", [D, 2, S])
        ek = sb("ek", [P, 2, GT, D])
        rk = sb("rk", [P, 2, GT, D])
        phik = sb("phik", [P, 2, GT, D])
        vx = sb("vx", [P, 2, GT, D + 1])
        KVm = sb("KVm", [P, 2, D + H])
        den = sb("den", [P, 2, GT, H])
        rden = sb("rden", [P, 2, GT, H])
        att = sb("att", [P, 2, GT, D])
        attT = sb("attT", [D, 2, S])
        qa = ysb[:, 0:FC * S // D, :].rearrange("p (c a) d -> p c (a d)", c=FC)
        qb = sb("qb", [P, FC, S])
        actT = sb("actT", [P, 2, FC, S])
        gelu_bias = sb("gelu_bias", [P, 1])

        bank = [ctx.enter_context(nc.psum_tensor(f"bank{i}", [P, 512], f32)) for i in range(8)]

        x_in = [sem(f"x_in{g}") for g in range(NG)]
        rw_in = sem("rw_in")
        eb_in = sem("eb_in")
        w_in = sem("w_in")
        ew_in = sem("ew_in")
        const_ready = sem("const_ready")
        pool_chain = sem("pool_chain")
        dve_chain = sem("dve_chain")
        ebias_ready = sem("ebias_ready")
        eb1_T = sem("eb1_T")
        stats_ready = sem("stats_ready")
        rstd_ready = sem("rstd_ready")
        xn_ready = sem("xn_ready")
        xn_stored = sem("xn_stored")
        xnT_ps = sem("xnT_ps")
        xnT_ready = sem("xnT_ready")
        logits_ps = sem("logits_ps")
        lg_ready = sem("lg_ready")
        ex_ready = sem("ex_ready")
        oh_ready = sem("oh_ready")
        rank_ps = sem("rank_ps")
        eid_ready = sem("eid_ready")
        pos_ready = sem("pos_ready")
        inq_ready = sem("inq_ready")
        inr_ready = sem("inr_ready")
        src_ps = sem("src_ps")
        src_ready = sem("src_ready")
        g_in = [sem(f"g_in{u}") for u in range(RING)]
        ewc_in = [sem(f"ewc_in{u}") for u in range(RING)]
        xg_T = sem("xg_T")
        xT_ready = sem("xT_ready")
        h_ps = sem("h_ps")
        hT_ready = sem("hT_ready")
        y_ps = sem("y_ps")
        y_ready = sem("y_ready")
        y_stored = sem("y_stored")
        yg_in = [sem(f"yg_in{g}") for g in range(NG)]
        h1_ready = sem("h1_ready")
        h1T_ps = sem("h1T_ps")
        h1T_ready = sem("h1T_ready")
        q_ps = sem("q_ps")
        k_ps = sem("k_ps")
        v_ps = sem("v_ps")
        q_out = sem("q_out")
        k_out = sem("k_out")
        v_out = sem("v_out")
        xi_ready = sem("xi_ready")
        phiq_ready = sem("phiq_ready")
        phik_ready = sem("phik_ready")
        ones_ready = sem("ones_ready")
        kvsum_ps = sem("kvsum_ps")
        KVm_ready = sem("KVm_ready")
        num_ps = sem("num_ps")
        att_ready = sem("att_ready")
        attT_ps = sem("attT_ps")
        attT_ready = sem("attT_ready")
        wo_ps = sem("wo_ps")
        x2_ready = sem("x2_ready")
        h2_ready = sem("h2_ready")
        h2T_ps = sem("h2T_ps")
        h2T_ready = sem("h2T_ready")
        u_ps = sem("u_ps")
        qa_ready = sem("qa_ready")
        qb_ready = sem("qb_ready")
        act_ready = sem("act_ready")
        w2_ps = sem("w2_ps")
        x3_ready = sem("x3_ready")
        res_ready = sem("res_ready")
        out_ready = sem("out_ready")
        out_done = sem("out_done")

        LN = ([("m0", g) for g in range(NG)] + [("a", 0), ("a", 1)]
              + [k for b in range(B) for k in [("l", b - 1)] * (b >= 1) + [("a", b + 2)] * (b + 2 < B)]
              + [("l", B - 1)] + [("m1", g) for g in range(NG)])
        LN_AT = {k: i + 1 for i, k in enumerate(LN)}
        slots = [len(range(u, NT, RING)) for u in range(RING)]
        LOOPS = (NT - 3) // RING

        class Tile:

            def __init__(self, i, n):
                self.slot, self.round = n % RING, i + n // RING
                self.k, self.parity = i * RING + n, n % 2

        def expert_tiles(eng, step, loops=LOOPS):
            with eng.Fori(0, loops) as i:
                for n in range(RING):
                    step(i, n)
            for k in range(loops * RING, NT):
                step(loops, k - loops * RING)

        def left(i, n):
            return not isinstance(i, int) or i * RING + n < NT

        def xn_bank(m, g):
            return 1 if m else g % 2

        block = ctx.enter_context(nc.Block())

        @block.sync
        def _(sp):
            for g in range(NG):
                sp.dma_start(x[:, g * GT:(g + 1) * GT, :], x_v[:, g * GT:(g + 1) * GT, :]).then_inc(x_in[g], 16)
            sp.dma_start(rw[:, :], rw_d).then_inc(rw_in, 16)
            sp.dma_start(rb[:, :], rb_d.unsqueeze(0).broadcast_to([P, NE])).then_inc(rw_in, 16)
            sp.dma_start(eb1r[:, :], eb1_d.rearrange("e (c p) -> (e c) p", p=P)).then_inc(eb_in, 16)
            sp.dma_start(ew[:, :, B2_AT:EW], eb2_d.unsqueeze(0).broadcast_to([P, NE, D])).then_inc(ew_in, 16)
            sp.dma_start(ew[:, :, W1_AT:W1_AT + F], ew1_d.rearrange("e p f -> p e f")).then_inc(ew_in, 16)
            for e in range(NE):
                sp.dma_start(ew[:, e, W2_AT:B1_AT].rearrange("p (c d) -> p c d", d=D),
                             ew2_d[e, :, :].rearrange("(c p) d -> p c d", p=P)).then_inc(ew_in, 16)
            for dst, src in ((wq[:, :], wq_d), (wkv[:, 0:D], wk_d), (wkv[:, D:2 * D], wv_d), (wo[:, :], wo_d),
                             (w1[:, :], w1_d), (w2[:, :, :], w2_d.rearrange("(c p) d -> p c d", p=P))):
                sp.dma_start(dst, src).then_inc(w_in, 16)
            for j, v in enumerate((g1_d, b1_d, g2_d, b2_d)):
                sp.dma_start(gb[:, j:j + 1], v.rearrange("(d a) -> d a", a=1)).then_inc(w_in, 16)
            for m in range(2):
                for g in range(NG):
                    sp.wait_ge(xn_ready, m * NG + g + 1)
                    sp.dma_start(xn_scr_v[:, g * GT:(g + 1) * GT, :],
                                 xn[:, g * GT:(g + 1) * GT, :]).then_inc(xn_stored, 16)

                def load_weights(i, n):
                    t = Tile(i, n)
                    e = sp.value_load(eid[0:1, bass.ds(t.k, 1)], min_val=0, max_val=NE - 1)
                    sp.dma_start(ewc[:, t.slot, :], ew[:, bass.ds(e, 1), :].squeeze(1)).then_inc(ewc_in[t.slot], 16)

                sp.wait_ge(eid_ready, m + 1)
                if m == 0:
                    sp.wait_ge(ew_in, 16 * (2 + NE))
                    sp.wait_ge(ebias_ready, 1)
                for n in range(RING):
                    load_weights(0, n)

                def step(i, n):
                    t = Tile(i, n)
                    sp.wait_ge(y_ready, m * NT + 1 + t.k)
                    if left(i, n + RING):
                        load_weights(i, n + RING)
                    sp.dma_start(y_scr_v[bass.ds(t.k, 1), :, :].squeeze(0),
                                 ysb[:, bass.ds(t.k, 1), :].squeeze(1)).then_inc(y_stored, 16)
                expert_tiles(sp, step, LOOPS - 1)
            for g in range(NG):
                sp.wait_ge(out_ready, g + 1)
                sp.dma_start(out_v[:, g * GT:(g + 1) * GT, :], x[:, g * GT:(g + 1) * GT, :]).then_inc(out_done, 16)
            sp.wait_ge(out_done, 16 * NG)

        @block.gpsimd
        def _(pool):
            chain = [0]

            def link(ins):
                chain[0] += 1
                ins.then_inc(pool_chain, 1)
                pool.wait_ge(pool_chain, chain[0])

            g = nc.gpsimd
            g.memset(ident[:, :], 0.0).then_inc(pool_chain, 1)
            g.memset(ones_bf[:, :], 1.0).then_inc(pool_chain, 1)
            g.memset(bmask[:, :, :], 1.0).then_inc(pool_chain, 1)
            g.memset(hmask[:, :], 1.0).then_inc(pool_chain, 1)
            g.memset(ltE[:, :, :], 1.0).then_inc(pool_chain, 1)
            g.memset(before[:, :], 1.0).then_inc(pool_chain, 1)
            chain[0] += 6
            g.memset(mhalf[:, :, :], -0.5).then_inc(const_ready, 1)
            pool.wait_ge(pool_chain, chain[0])
            g.affine_select(out=ident[:, :], in_=ident[:, :], compare_op=ALU.not_equal, fill=1.0, base=0,
                            pattern=[[-1, P]], channel_multiplier=1).then_inc(const_ready, 1)

            def normaliser(at):
                kind, n = LN[at]
                pool.wait_ge(stats_ready, at + 1)
                a = at % 2
                v = mv[:, n * GT:(n + 1) * GT, 1:2]
                g.tensor_scalar(vin[:, a, :, 0:1], v, 1.0, EPS, ALU.mult, ALU.add).then_inc(pool_chain, 1)
                g.tensor_scalar(vin[:, a, :, 1:2], v, 1.0 + EPS, EPS * EPS, ALU.mult, ALU.add).then_inc(pool_chain, 1)
                chain[0] += 2
                pool.wait_ge(pool_chain, chain[0])
                wide = 2 if kind == "a" else 1
                g.tensor_tensor(out=rstd[:, n * GT:(n + 1) * GT, 0:wide], in0=vin[:, a, :, 0:wide],
                                in1=mhalf[:, :, 0:wide], op=ALU.pow).then_inc(rstd_ready, 1)

            pool.wait_ge(const_ready, 2)
            for at in range(NG):
                normaliser(at)
            g.affine_select(out=before[:, :], in_=before[:, :], compare_op=ALU.is_gt, fill=0.0, base=0,
                            pattern=[[1, P]], channel_multiplier=-1).then_inc(const_ready, 1)
            g.affine_select(out=ltE[:, :, :], in_=ltE[:, :, :], compare_op=ALU.is_gt, fill=0.0, base=0,
                            pattern=[[1, NE], [-1, NE]], channel_multiplier=0).then_inc(const_ready, 1)
            g.iota(prefer[:, :], [[-1, NE]], base=NE, channel_multiplier=0,
                   allow_small_or_imprecise_dtypes=True).then_inc(const_ready, 1)
            g.iota(rowid[:, :], [[1, P]], base=0, channel_multiplier=0,
                   allow_small_or_imprecise_dtypes=True).then_inc(const_ready, 1)
            g.iota(tileid[:, :], [[1, NT]], base=0, channel_multiplier=0,
                   allow_small_or_imprecise_dtypes=True).then_inc(const_ready, 1)
            g.iota(tokbase[:, :], [[P, T]], base=0, channel_multiplier=0,
                   allow_small_or_imprecise_dtypes=True).then_inc(const_ready, 1)
            g.iota(pcol[:, :], [[0, 1]], base=0, channel_multiplier=1,
                   allow_small_or_imprecise_dtypes=True).then_inc(const_ready, 1)
            for m_, pat in ((bmask[:, :, :], [[-DH, H], [0, DH]]), (hmask[:, :], [[-DH, H]])):
                link(g.affine_select(out=m_, in_=m_, compare_op=ALU.is_ge, fill=0.0, base=0,
                                     pattern=pat, channel_multiplier=1))
                g.affine_select(out=m_, in_=m_, compare_op=ALU.is_ge, fill=0.0, base=DH - 1,
                                pattern=[[-s_, n_] for s_, n_ in pat], channel_multiplier=-1).then_inc(const_ready, 1)
            g.memset(gelu_bias[:, :], -0.1 * HALF).then_inc(const_ready, 1)
            g.memset(vx[:, :, :, D:D + 1], 1.0).then_inc(ones_ready, 1)

            def gather_tokens(m):
                pool.wait_ge(xn_stored, 16 * NG * (m + 1))
                pool.wait_ge(src_ready, m + 1)
                for k in range(NT):
                    if k >= RING:
                        pool.wait_ge(xg_T, m * NT + k - RING + 1)
                    g.indirect_dma_start(out=Xg[:, k % RING, :], out_offset=None, in_=xn_scr,
                                         in_offset=bass.IndirectOffsetOnAxis(ap=srcu[:, k:k + 1], axis=0)
                                         ).then_inc(g_in[k % RING], 16)

            def gather_results(m, group):
                for t in range(group * GT, (group + 1) * GT):
                    g.indirect_dma_start(out=Yg[:, t, :], out_offset=None, in_=y_scr,
                                         in_offset=bass.IndirectOffsetOnAxis(ap=posu[:, t:t + 1], axis=0)
                                         ).then_inc(yg_in[t // GT], 16)

            def attention_input(b):
                normaliser(LN_AT["a", b] - 1)
                pool.wait_ge(rstd_ready, LN_AT["a", b])
                for j in range(GT):
                    t = b * GT + j
                    last = g.tensor_scalar(xi[:, t, :], x[:, t, :], mv[:, t, 0:1], rstd[:, t, 0:1],
                                           ALU.subtract, ALU.mult)
                last.then_inc(xi_ready, 1)

            def residuals(b):
                pool.wait_ge(h2_ready, b + 1)
                g.tensor_tensor(out=xi[:, b * GT:(b + 1) * GT, :], in0=xi[:, b * GT:(b + 1) * GT, :],
                                in1=x[:, b * GT:(b + 1) * GT, :], op=ALU.add).then_inc(res_ready, 1)

            gather_tokens(0)
            pool.wait_ge(y_stored, 16 * NT)
            gather_results(0, 0)
            gather_results(0, 1)
            for kind, n in LN[NG:NG + 2 * B]:
                if kind == "a":
                    attention_input(n)
                    if n + 2 < NG:
                        gather_results(0, n + 2)
                else:
                    normaliser(LN_AT[kind, n] - 1)
            residuals(0)
            for b in range(B):
                if b + 1 < B:
                    residuals(b + 1)
                normaliser(LN_AT["m1", b] - 1)
            gather_tokens(1)
            pool.wait_ge(y_stored, 16 * NT * 2)
            for group in range(NG):
                gather_results(1, group)

        @block.scalar
        def _(act):
            A = nc.scalar.activation

            def take_xn(m, g):
                act.wait_ge(xnT_ps, m * NG + g + 1)
                A(xnT[:, g * GT:(g + 1) * GT, :], bank[xn_bank(m, g)][:, :], ACT.Copy).then_inc(xnT_ready, 1)

            def exponentials(m):
                act.wait_ge(lg_ready, NG * (m + 1))
                A(ex[:, :, :], lg[:, :, :], ACT.Exp).then_inc(ex_ready, 1)

            def experts(m):
                def step(i, n):
                    t = Tile(i, n)
                    act.wait_ge(h_ps, m * NT + 1 + t.k)
                    for c in range(FC):
                        last = A(hT[:, t.slot, c * P:(c + 1) * P], bank[2 + t.parity][:, c * P:(c + 1) * P],
                                 ACT.Relu, bias=ewc[:, t.slot, B1_AT + c:B1_AT + c + 1])
                    last.then_inc(hT_ready, 1)
                expert_tiles(act, step)

            for g in range(NG):
                take_xn(0, g)
            exponentials(0)
            experts(0)
            act.wait_ge(w_in, 16 * 10)
            act.wait_ge(ones_ready, 1)

            def norm1(b):
                act.wait_ge(h1T_ps, b + 1)
                A(h1T[:, b % 2, :], bank[0][:, :], ACT.Identity, scale=gb[:, 0:1], bias=gb[:, 1:2]
                  ).then_inc(h1T_ready, 1)

            def take_kv(b):
                s = b % 2
                act.wait_ge(k_ps, b + 1)
                A(ek[:, s, :, :], bank[3][:, :].rearrange("p (t d) -> p t d", d=D), ACT.Exp)
                A(rk[:, s, :, :], bank[3][:, :].rearrange("p (t d) -> p t d", d=D), ACT.Relu).then_inc(k_out, 1)
                act.wait_ge(v_ps, b + 1)
                A(vx[:, s, :, 0:D], bank[4][:, :].rearrange("p (t d) -> p t d", d=D), ACT.Copy).then_inc(v_out, 1)

            def take_q(b):
                s = b % 2
                act.wait_ge(q_ps, b + 1)
                A(eq[:, s, :], bank[2][:, :], ACT.Exp)
                A(rq[:, s, :], bank[2][:, :], ACT.Relu).then_inc(q_out, 1)

            norm1(0)
            take_kv(0)
            take_q(0)
            for b in range(B):
                if b + 1 < B:
                    norm1(b + 1)
                    take_kv(b + 1)
                act.wait_ge(attT_ps, b + 1)
                A(attT[:, b % 2, :], bank[1][:, :], ACT.Copy).then_inc(attT_ready, 1)
                if b + 1 < B:
                    take_q(b + 1)

            def norm2(b):
                act.wait_ge(h2T_ps, b + 1)
                A(h1T[:, b % 2, :], bank[0][:, :], ACT.Identity, scale=gb[:, 2:3], bias=gb[:, 3:4]
                  ).then_inc(h2T_ready, 1)

            def lookup(b):
                for c in range(FC):
                    act.wait_ge(qb_ready, b * FC + c + 1)
                    level = qb[:, c, :].bitcast(i16).rearrange("p (n two) -> p n two", two=2)[:, :, 0]
                    A(actT[:, b % 2, c, :], level, ACT.Gelu_apprx_tanh, scale=0.1,
                      bias=gelu_bias[:, 0:1]).then_inc(act_ready, 1)

            norm2(0)
            lookup(0)
            norm2(1)
            for b in range(B):
                if b + 1 < B:
                    lookup(b + 1)
                if b >= 1:
                    take_xn(1, b - 1)
                if b + 2 < B:
                    norm2(b + 2)
            take_xn(1, NG - 1)
            exponentials(1)
            experts(1)

        @block.tensor
        def _(pe):
            mm = nc.tensor.matmul

            pe.wait_ge(eb_in, 16)
            pe.wait_ge(const_ready, 2)
            nc.tensor.transpose(bank[7][:, 0:NE * FC], eb1r[:, :], ident[0:NE * FC, 0:NE * FC]).then_inc(eb1_T, 1)
            pe.wait_ge(rw_in, 32)

            def turn_xn(m, g):
                pe.wait_ge(xn_ready, m * NG + g + 1)
                if g >= 2 - m:
                    pe.wait_ge(xnT_ready, m * NG + g - 1 + m)
                for j in range(GT):
                    last = nc.tensor.transpose(bank[xn_bank(m, g)][:, j * P:(j + 1) * P], xn[:, g * GT + j, :],
                                               ident[:, :])
                last.then_inc(xnT_ps, 1)

            def logits(m, g):
                pe.wait_ge(xnT_ready, m * NG + g + 1)
                if m * NG + g >= 1:
                    pe.wait_ge(lg_ready, m * NG + g)
                for j in range(GT):
                    last = mm(bank[5][:, j * NE:(j + 1) * NE], xnT[:, g * GT + j, :], rw[:, :], start=True, stop=True)
                last.then_inc(logits_ps, 1)

            def ranks(m):
                R = bank[3]
                pe.wait_ge(oh_ready, NG * (m + 1))
                pe.wait_ge(const_ready, 12)

                def spread(t):
                    n = T - t
                    return bc(oh[:, t, :].unsqueeze(1), [P, n, NE])

                mm(R[:, NE:(T + 1) * NE], ones_bf[:, :], spread(0), start=True, stop=False, skip_group_check=True)
                mm(R[:, 0:NE], before[:, :], oh[:, 0, :], start=False, stop=False, skip_group_check=True)
                mm(R[:, NE:T * NE], before[:, :], oh[:, 1:T, :], start=False, stop=False, skip_group_check=True)
                for t in range(1, T):
                    last = mm(R[:, (t + 1) * NE:(T + 1) * NE], ones_bf[:, :], spread(t),
                              start=False, stop=t == T - 1, skip_group_check=True)
                last.then_inc(rank_ps, 1)

            def sources(m):
                pe.wait_ge(inq_ready, m + 1)
                for t in range(T):
                    pe.wait_ge(inr_ready, m * T + t + 1)
                    mm(bank[4][:, 0:NT], inr[:, t, :], inqt[:, t, :], start=t == 0, stop=False)
                    last = mm(bank[4][:, 0:NT], inr[:, t, :], inqp[:, t, :], start=False, stop=t == T - 1)
                last.then_inc(src_ps, 1)

            def experts(m):
                def turn(i, n):
                    t = Tile(i, n)
                    pe.wait_ge(g_in[t.slot], 16 * (m * slots[t.slot] + 1 + t.round))
                    nc.tensor.transpose(bank[t.parity][:, 0:P], Xg[:, t.slot, :], ident[:, :]).then_inc(xg_T, 1)

                def up(i, n):
                    t = Tile(i, n)
                    pe.wait_ge(ewc_in[t.slot], 16 * (m * slots[t.slot] + 1 + t.round))
                    pe.wait_ge(xT_ready, m * NT + 1 + t.k)
                    for c in range(FC):
                        last = mm(bank[2 + t.parity][:, c * P:(c + 1) * P], ewc[:, t.slot, c * P:(c + 1) * P],
                                  xT[:, t.slot, :], start=True, stop=True)
                    last.then_inc(h_ps, 1)

                def down(i, n):
                    t = Tile(i, n)
                    pe.wait_ge(hT_ready, m * NT + 1 + t.k)
                    if not left(i, n + 1):
                        pe.wait_ge(y_ready, m * NT + t.k - 1)
                    for c in range(FC):
                        last = mm(bank[4 + t.parity][:, 0:D], hT[:, t.slot, c * P:(c + 1) * P],
                                  ewc[:, t.slot, W2_AT + c * D:W2_AT + (c + 1) * D], start=c == 0, stop=c == FC - 1)
                    last.then_inc(y_ps, 1)

                turn(0, 0)
                turn(0, 1)
                up(0, 0)

                def step(i, n):
                    if left(i, n + 2):
                        turn(i, n + 2)
                    if left(i, n + 1):
                        up(i, n + 1)
                    down(i, n)
                expert_tiles(pe, step)

            turn_xn(0, 0)
            for g in range(NG):
                if g + 1 < NG:
                    turn_xn(0, g + 1)
                logits(0, g)
            ranks(0)
            sources(0)
            experts(0)
            pe.wait_ge(w_in, 16 * 10)

            def turn1(b):
                pe.wait_ge(h1_ready, b + 1)
                for j in range(GT):
                    last = nc.tensor.transpose(bank[0][:, j * P:(j + 1) * P], h1[:, b % 2, j, :], ident[:, :])
                last.then_inc(h1T_ps, 1)

            def keys_values(b):
                pe.wait_ge(h1T_ready, b + 1)
                if b >= 1:
                    pe.wait_ge(v_out, b)
                for bk, at, done in ((3, 0, k_ps), (4, D, v_ps)):
                    for j in range(GT):
                        last = mm(bank[bk][:, j * D:(j + 1) * D], h1T[:, b % 2, j * P:(j + 1) * P],
                                  wkv[:, at:at + D], start=True, stop=True)
                    last.then_inc(done, 1)

            def queries(b):
                if b >= 1:
                    pe.wait_ge(q_out, b)
                mm(bank[2][:, :], wq[:, :], h1T[:, b % 2, :], start=True, stop=True).then_inc(q_ps, 1)

            def sum_kv(b):
                s = b % 2
                pe.wait_ge(phik_ready, b + 1)
                pe.wait_ge(v_out, b + 1)
                for j in range(GT):
                    last = mm(bank[5][:, 0:D + 1], phik[:, s, j, :], vx[:, s, j, :], start=j == 0, stop=j == GT - 1)
                last.then_inc(kvsum_ps, 1)

            def numerators(b):
                s = b % 2
                pe.wait_ge(KVm_ready, b + 1)
                pe.wait_ge(phiq_ready, b + 1)
                if b >= 1:
                    pe.wait_ge(x2_ready, b)
                for j in range(GT):
                    last = mm(bank[6 + j // 2][:, (j % 2) * (D + H):(j % 2 + 1) * (D + H)],
                              phiq[:, s, j * P:(j + 1) * P], KVm[:, s, :], start=True, stop=True)
                last.then_inc(num_ps, 1)

            def turn_att(b):
                pe.wait_ge(att_ready, b + 1)
                for j in range(GT):
                    last = nc.tensor.transpose(bank[1][:, j * P:(j + 1) * P], att[:, b % 2, j, :], ident[:, :])
                last.then_inc(attT_ps, 1)

            def project(b):
                pe.wait_ge(attT_ready, b + 1)
                for j in range(GT):
                    last = mm(bank[6][:, j * P:(j + 1) * P], attT[:, b % 2, j * P:(j + 1) * P], wo[:, :],
                              start=True, stop=True)
                last.then_inc(wo_ps, 1)

            turn1(0)
            keys_values(0)
            queries(0)
            for b in range(B):
                more = b + 1 < B
                sum_kv(b)
                if more:
                    turn1(b + 1)
                numerators(b)
                if more:
                    keys_values(b + 1)
                turn_att(b)
                if more:
                    queries(b + 1)
                project(b)

            def turn2(b):
                pe.wait_ge(h2_ready, b + 1)
                if b >= 1:
                    pe.wait_ge(h2T_ready, b)
                for j in range(GT):
                    last = nc.tensor.transpose(bank[0][:, j * P:(j + 1) * P], h1[:, b % 2, j, :], ident[:, :])
                last.then_inc(h2T_ps, 1)

            def up2(b):
                pe.wait_ge(h2T_ready, b + 1)
                for c in range(FC):
                    n = b * FC + c
                    if n >= 3:
                        pe.wait_ge(qa_ready, n - 2)
                    mm(bank[2 + n % 3][:, :], w1[:, c * P:(c + 1) * P], h1T[:, b % 2, :], start=True, stop=True
                       ).then_inc(u_ps, 1)

            def down2(b):
                if b >= 2:
                    pe.wait_ge(x3_ready, b - 1)
                pe.wait_ge(act_ready, (b + 1) * FC)
                for j in range(GT):
                    for c in range(FC):
                        last = mm(bank[6 + b % 2][:, j * P:(j + 1) * P], actT[:, b % 2, c, j * P:(j + 1) * P],
                                  w2[:, c, :], start=c == 0, stop=c == FC - 1)
                last.then_inc(w2_ps, 1)

            turn2(0)
            up2(0)
            for b in range(B):
                if b + 1 < B:
                    turn2(b + 1)
                    up2(b + 1)
                down2(b)
                if b >= 1:
                    turn_xn(1, b - 1)
                    logits(1, b - 1)
            turn_xn(1, NG - 1)
            logits(1, NG - 1)
            ranks(1)
            sources(1)
            experts(1)

        @block.vector
        def _(dve):
            chain = [0]
            v = nc.vector

            def link(ins):
                chain[0] += 1
                ins.then_inc(dve_chain, 1)
                dve.wait_ge(dve_chain, chain[0])

            def statistics(kind, n, src):
                for j in range(GT):
                    last = v.bn_stats(stat[:, j, :], src[:, n * GT + j, :])
                link(last)
                for j in range(GT):
                    last = v.bn_aggr(mv[:, n * GT + j, :], stat[:, j, :])
                last.then_inc(stats_ready, 1)
                dve.wait_ge(stats_ready, LN_AT[kind, n])

            def normalise(dst, src, n, which=0):
                for j in range(GT):
                    t = n * GT + j
                    last = v.tensor_scalar(dst(j), src[:, t, :], mv[:, t, 0:1], rstd[:, t, which:which + 1],
                                           ALU.subtract, ALU.mult)
                return last

            def pick(m, g):
                ts = slice(g * GT, (g + 1) * GT)
                dve.wait_ge(logits_ps, m * NG + g + 1)
                link(v.tensor_tensor(out=lg[:, ts, :], in0=bank[5][:, 0:GT * NE].rearrange("p (t e) -> p t e", e=NE),
                                     in1=bc(rb[:, :].unsqueeze(1), [P, GT, NE]), op=ALU.add))
                link(v.tensor_reduce(lmax[:, ts], lg[:, ts, :], AX, ALU.max))
                v.tensor_tensor(out=lg[:, ts, :], in0=lg[:, ts, :], in1=bc(lmax[:, ts].unsqueeze(2), [P, GT, NE]),
                                op=ALU.subtract).then_inc(lg_ready, 1)
                dve.wait_ge(lg_ready, m * NG + g + 1)
                if m == 0 and g == 0:
                    dve.wait_ge(const_ready, 12)
                link(v.scalar_tensor_tensor(out=key[:, ts, :], in0=lg[:, ts, :], scalar=0.0,
                                            in1=bc(prefer[:, :].unsqueeze(1), [P, GT, NE]),
                                            op0=ALU.is_ge, op1=ALU.mult))
                link(v.tensor_reduce(kmax[:, ts], key[:, ts, :], AX, ALU.max))
                v.tensor_tensor(out=oh[:, ts, :], in0=key[:, ts, :], in1=bc(kmax[:, ts].unsqueeze(2), [P, GT, NE]),
                                op=ALU.is_equal).then_inc(oh_ready, 1)

            def gates(m):
                dve.wait_ge(ex_ready, m + 1)
                link(v.tensor_reduce(psum_e[:, :], ex[:, :, :], AX, ALU.add))
                link(v.reciprocal(gate[:, :], psum_e[:, :]))
                link(v.tensor_scalar(gate[:, :], gate[:, :], 0.5, None, ALU.mult))

            def route(m):
                dve.wait_ge(oh_ready, NG * (m + 1))
                dve.wait_ge(rank_ps, m + 1)
                R = bank[3]
                link(v.tensor_scalar(ncnt[:, :], R[:, T * NE:(T + 1) * NE], 1.0 / P, (P - 1.0) / P - 0.498046875,
                                     ALU.mult, ALU.add))
                link(v.tensor_scalar(cnt[:, :], ncnt[:, :], MAGIC, MAGIC, ALU.add, ALU.subtract))
                link(v.tensor_tensor(out=cm[:, :, :], in0=bc(cnt[:, :].unsqueeze(1), [P, NE, NE]), in1=ltE[:, :, :],
                                     op=ALU.mult))
                link(v.tensor_reduce(sx[:, :], cm[:, :, :], AX, ALU.add))
                link(v.tensor_tensor(out=send[:, :], in0=sx[:, :], in1=cnt[:, :], op=ALU.add))
                link(v.scalar_tensor_tensor(out=v3[:, :, :], in0=bc(sx[:, :].unsqueeze(1), [P, T, NE]), scalar=float(P),
                                            in1=R[:, 0:T * NE].rearrange("p (t e) -> p t e", e=NE),
                                            op0=ALU.mult, op1=ALU.add))
                link(v.tensor_tensor(out=v3[:, :, :], in0=v3[:, :, :], in1=oh[:, :, :], op=ALU.mult))
                link(v.tensor_reduce(pos[:, :], v3[:, :, :], AX, ALU.add))
                link(v.tensor_scalar(qf[:, :], pos[:, :], 1.0 / P, -0.498046875, ALU.mult, ALU.add))
                link(v.tensor_scalar(qf[:, :], qf[:, :], MAGIC, MAGIC, ALU.add, ALU.subtract))
                link(v.scalar_tensor_tensor(out=rf[:, :], in0=qf[:, :], scalar=-float(P), in1=pos[:, :],
                                            op0=ALU.mult, op1=ALU.add))
                link(v.tensor_tensor(out=inq[:, :, :], in0=bc(tileid[:, :].unsqueeze(1), [P, T, NT]),
                                     in1=bc(qf[:, :].unsqueeze(2), [P, T, NT]), op=ALU.is_equal))
                v.tensor_tensor(out=inqt[:, :, :], in0=inq[:, :, :], in1=bc(tokbase[:, :].unsqueeze(2), [P, T, NT]),
                                op=ALU.mult)
                v.tensor_scalar(inqp[:, :, :], inq[:, :, :], pcol[:, 0:1], None, ALU.mult).then_inc(inq_ready, 1)
                for t in range(T):
                    v.tensor_scalar(inr[:, t, :], rowid[:, :], rf[:, t:t + 1], None, ALU.is_equal).then_inc(inr_ready, 1)
                link(v.tensor_tensor(out=ek_c[:, :, :], in0=bc(tileid[:, :].unsqueeze(2), [P, NT, NE]),
                                     in1=bc(send[:, :].unsqueeze(1), [P, NT, NE]), op=ALU.is_ge))
                link(v.tensor_reduce(eidf[:, :], ek_c[:, :, :], AX, ALU.add))
                v.tensor_scalar(eid[:, :], eidf[:, :], NE - 1.0, None, ALU.min).then_inc(eid_ready, 1)
                v.tensor_copy(posu[:, :], pos[:, :]).then_inc(pos_ready, 1)
                dve.wait_ge(src_ps, m + 1)
                v.tensor_copy(srcu[:, :], bank[4][:, 0:NT]).then_inc(src_ready, 1)
                gates(m)

            def experts(m):
                def take_x(i, n):
                    t = Tile(i, n)
                    dve.wait_ge(xg_T, m * NT + 1 + t.k)
                    v.tensor_copy(xT[:, t.slot, :], bank[t.parity][:, 0:P]).then_inc(xT_ready, 1)

                def take_y(i, n):
                    t = Tile(i, n)
                    dve.wait_ge(y_ps, m * NT + 1 + t.k)
                    v.tensor_tensor(out=ysb[:, bass.ds(t.k, 1), :].squeeze(1), in0=bank[4 + t.parity][:, 0:D],
                                    in1=ewc[:, t.slot, B2_AT:EW], op=ALU.add).then_inc(y_ready, 1)

                take_x(0, 0)
                take_x(0, 1)

                def step(i, n):
                    if left(i, n + 2):
                        take_x(i, n + 2)
                    take_y(i, n)
                expert_tiles(dve, step)

            def combine(m, g):
                dve.wait_ge(yg_in[g], 16 * GT * (m + 1))
                for t in range(g * GT, (g + 1) * GT):
                    last = v.scalar_tensor_tensor(out=x[:, t, :], in0=Yg[:, t, :], scalar=gate[:, t:t + 1],
                                                  in1=x[:, t, :], op0=ALU.mult, op1=ALU.add)
                return last

            for g in range(NG):
                dve.wait_ge(x_in[g], 16)
                statistics("m0", g, x)
            def renormalise(m, g):
                dve.wait_ge(rstd_ready, LN_AT[f"m{m}", g])
                normalise(lambda j: xn[:, g * GT + j, :], x, g).then_inc(xn_ready, 1)

            for g in range(NG):
                renormalise(0, g)
            dve.wait_ge(eb1_T, 1)
            v.tensor_copy(ew[:, :, B1_AT:B2_AT], bank[7][:, 0:NE * FC].rearrange("p (e c) -> p e c", c=FC)
                          ).then_inc(ebias_ready, 1)
            for g in range(NG):
                pick(0, g)
            route(0)
            experts(0)

            def begin(b):
                link(combine(0, b))
                statistics("a", b, x)

            def norm1(b):
                dve.wait_ge(rstd_ready, LN_AT["a", b])
                normalise(lambda j: h1[:, b % 2, j, :], x, b, 1).then_inc(h1_ready, 1)

            def phi(dst, e, r, done):
                v.scalar_tensor_tensor(out=dst, in0=e, scalar=1.0, in1=r, op0=ALU.min, op1=ALU.add).then_inc(done, 1)

            def phi_k(b):
                s = b % 2
                dve.wait_ge(k_out, b + 1)
                phi(phik[:, s, :, :], ek[:, s, :, :], rk[:, s, :, :], phik_ready)

            def phi_q(b):
                s = b % 2
                dve.wait_ge(q_out, b + 1)
                phi(phiq[:, s, :], eq[:, s, :], rq[:, s, :], phiq_ready)

            def mask_kv(b):
                s = b % 2
                dve.wait_ge(kvsum_ps, b + 1)
                v.tensor_tensor(out=KVm[:, s, 0:D], in0=bank[5][:, 0:D], in1=bmask[:, :, :].rearrange("p h e -> p (h e)"),
                                op=ALU.mult)
                v.tensor_scalar(KVm[:, s, D:D + H], hmask[:, :], bank[5][:, D:D + 1], None, ALU.mult
                                ).then_inc(KVm_ready, 1)

            def divide(b):
                s = b % 2
                dve.wait_ge(num_ps, b + 1)
                nd = [bank[6 + j][:, 0:2 * (D + H)].rearrange("p (t n) -> p t n", t=2) for j in range(2)]
                for j in range(2):
                    last = v.tensor_scalar(den[:, s, 2 * j:2 * j + 2, :], nd[j][:, :, D:D + H], 1e-6, None, ALU.add)
                link(last)
                link(v.reciprocal(rden[:, s, :, :], den[:, s, :, :]))
                for j in range(2):
                    ts = slice(2 * j, 2 * j + 2)
                    last = v.tensor_tensor(
                        out=att[:, s, ts, :].rearrange("p t (h e) -> p t h e", e=DH),
                        in0=nd[j][:, :, 0:D].rearrange("p t (h e) -> p t h e", e=DH),
                        in1=bc(rden[:, s, ts, :].unsqueeze(3), [P, 2, H, DH]), op=ALU.mult)
                last.then_inc(att_ready, 1)

            def residual(b):
                dve.wait_ge(wo_ps, b + 1)
                dve.wait_ge(xi_ready, b + 1)
                xb = xi[:, b * GT:(b + 1) * GT, :]
                v.tensor_tensor(out=xb, in0=bank[6][:, :].rearrange("p (t d) -> p t d", d=D), in1=xb, op=ALU.add
                                ).then_inc(x2_ready, 1)

            def begin2(b):
                dve.wait_ge(x2_ready, b + 1)
                statistics("l", b, xi)

            begin(0)
            begin(1)
            norm1(0)
            norm1(1)
            phi_k(0)
            phi_q(0)
            for b in range(B):
                mask_kv(b)
                if b >= 1:
                    begin2(b - 1)
                if b + 2 < B:
                    begin(b + 2)
                divide(b)
                if b + 2 < B:
                    norm1(b + 2)
                if b + 1 < B:
                    phi_k(b + 1)
                residual(b)
                if b + 1 < B:
                    phi_q(b + 1)
            begin2(B - 1)

            def norm2(b):
                dve.wait_ge(rstd_ready, LN_AT["l", b])
                normalise(lambda j: h1[:, b % 2, j, :], xi, b).then_inc(h2_ready, 1)

            def quantise(b):
                for c in range(FC):
                    n = b * FC + c
                    dve.wait_ge(u_ps, n + 1)
                    v.tensor_scalar(qa[:, c, :], bank[2 + n % 3][:, :], 10.0, QBASE + HALF, ALU.mult, ALU.add
                                    ).then_inc(qa_ready, 1)
                    dve.wait_ge(qa_ready, n + 1)
                    if b >= 1:
                        dve.wait_ge(act_ready, n - FC + 1)
                    v.tensor_scalar(qb[:, c, :], qa[:, c, :], QBASE, QBASE + LEVELS - 1, ALU.max, ALU.min
                                    ).then_inc(qb_ready, 1)

            norm2(0)
            norm2(1)
            quantise(0)
            for b in range(B):
                if b + 1 < B:
                    quantise(b + 1)
                if b >= 2:
                    pick(1, b - 2)
                if b >= 1:
                    renormalise(1, b - 1)
                dve.wait_ge(w2_ps, b + 1)
                dve.wait_ge(res_ready, b + 1)
                v.tensor_tensor(out=x[:, b * GT:(b + 1) * GT, :],
                                in0=bank[6 + b % 2][:, :].rearrange("p (t d) -> p t d", d=D),
                                in1=xi[:, b * GT:(b + 1) * GT, :], op=ALU.add).then_inc(x3_ready, 1)
                dve.wait_ge(x3_ready, b + 1)
                statistics("m1", b, x)
                if b + 2 < B:
                    norm2(b + 2)
            pick(1, NG - 2)
            renormalise(1, NG - 1)
            pick(1, NG - 1)

            route(1)
            experts(1)
            for g in range(NG):
                combine(1, g).then_inc(out_ready, 1)


_INS = ['L0_attn_x', 'L0_attn_ln1_g', 'L0_attn_ln1_b', 'L0_attn_wq', 'L0_attn_wk', 'L0_attn_wv', 'L0_attn_wo',
        'L0_attn_ln2_g', 'L0_attn_ln2_b', 'L0_attn_w1', 'L0_attn_w2', 'L0_ffn_router_W', 'L0_ffn_router_b',
        'L0_ffn_W1', 'L0_ffn_b1', 'L0_ffn_W2', 'L0_ffn_b2']
_OUTS = [((B, S, D), 'float32')]


def kernel(**inputs):
    import numpy as _np
    import concourse.bacc as _bacc
    from concourse import mybir as _mybir
    from concourse.bass_utils import run_bass_kernel_spmd as _run

    nc = _bacc.Bacc("TRN2", target_bir_lowering=False, num_devices=1)
    arrays, args = {}, []
    for name in _INS:
        a = _np.ascontiguousarray(inputs[name])
        arrays[f"in_{name}_dram"] = a
        args.append(nc.dram_tensor(f"in_{name}_dram", a.shape, _mybir.dt.from_np(a.dtype), kind="ExternalInput").ap())
    for i, (shape, dtype) in enumerate(_OUTS):
        dt = _mybir.dt.from_np(_np.dtype(dtype))
        args.append(nc.dram_tensor(f"out_{i}_dram", shape, dt, kind="ExternalOutput").ap())
    macaron_kernel(nc, *args)
    r = _run(nc, [arrays], core_ids=[0])
    got = tuple(r.results[0][f"out_{i}_dram"] for i in range(len(_OUTS)))
    return got[0]
```

```python
import numpy as np
import concourse.bass as bass
from concourse import mybir
from contextlib import ExitStack

P = 128
D = 128
B = 4
S = 512
TOK = B * S
T = TOK // P
GT = S // P
NG = T // GT
NE = 8
F = 512
FC = F // P
H = 16
DH = D // H
LEVELS = 256
HALF = LEVELS // 2
NT = (TOK + NE * (P - 1)) // P
UNROLL = 8
RING = 4
FIRST = 2
AHEAD = UNROLL + 2
LAST_BY_ACT = (2, 3)
POOL_GROUP = 1
WARM_START, WARM_FRONT, WARM_ROUTE, WARM_GATHER, WARM_STEP, WARM_TAIL = 14, 6, 16, 14, 6, 10
EPS = 1e-5
MAGIC = 1.5 * 2.0 ** 23
QBASE = 2.0 ** 23
W1_AT, W2_AT, B1_AT, B2_AT, EW = 0, F, F + FC * D, F + FC * D + FC, F + FC * D + FC + D


def bc(ap, shape):
    return ap.broadcast_to(list(shape))


def macaron_kernel(nc, x_d, g1_d, b1_d, wq_d, wk_d, wv_d, wo_d, g2_d, b2_d, w1_d, w2_d,
                   rw_d, rb_d, ew1_d, eb1_d, ew2_d, eb2_d, out_d):
    f32, bf16, f16 = mybir.dt.float32, mybir.dt.bfloat16, mybir.dt.float16
    i16, i32, u32 = mybir.dt.int16, mybir.dt.int32, mybir.dt.uint32
    ALU, ACT, AX = mybir.AluOpType, mybir.ActivationFunctionType, mybir.AxisListType.X

    x_v = x_d.rearrange("b (t p) d -> p (b t) d", p=P)
    out_v = out_d.rearrange("b (t p) d -> p (b t) d", p=P)
    xn_scr = nc.dram_tensor("xn_scratch", [TOK, D], f32, kind="Internal").ap()
    y_scr = nc.dram_tensor("y_scratch", [TOK + NT * P, D], f32, kind="Internal").ap()
    xn_scr_v = xn_scr.rearrange("(t p) d -> p t d", p=P)
    y_scr_v = y_scr[0:TOK, :].rearrange("(t p) d -> p t d", p=P)

    ctx = ExitStack()
    with ctx:
        def sb(name, shape, dt=f32):
            return ctx.enter_context(nc.sbuf_tensor(name, shape, dt))

        def sem(name):
            return ctx.enter_context(nc.semaphore(name))

        x = sb("x", [P, T, D])
        xi = sb("xi", [P, T, D])
        xn = sb("xn", [P, T, D])
        stat = sb("stat", [P, GT, 6])
        mv = sb("mv", [P, T, 2])
        vin = sb("vin", [P, 2, GT, 2])
        rstd = sb("rstd", [P, T, 2])
        nmean = sb("nmean", [P, 2, GT, 1])
        shift = sb("shift", [P, T, 2])
        wq = sb("wq", [D, D])
        wkv = sb("wkv", [D, 2 * D])
        wo = sb("wo", [D, D])
        w1 = sb("w1", [D, F])
        w2 = sb("w2", [P, FC, D])
        rw = sb("rw", [D, NE])
        rb = sb("rb", [P, NE])
        gb = sb("gb", [D, 4])
        eb1r = sb("eb1r", [NE * FC, P])
        ew = sb("ew", [P, NE, EW])
        ident = sb("ident", [P, P])
        ones_bf = sb("ones_bf", [P, P], bf16)
        before = sb("before", [P, P], bf16)
        bmask = sb("bmask", [P, H, DH])
        hmask = sb("hmask", [P, H])
        prefer = sb("prefer", [P, NE])
        ltE = sb("ltE", [P, NE, NE])
        rowid = sb("rowid", [P, P], f16)
        tileid = sb("tileid", [P, NT])
        token1 = sb("token1", [P, T])
        padrow = sb("padrow", [P, NT])
        mhalf = sb("mhalf", [P, GT, 2])
        xnT = sb("xnT", [D, T, P])
        lg = sb("lg", [P, T, NE])
        lmax = sb("lmax", [P, T])
        ex = sb("ex", [P, T, NE])
        key = sb("key", [P, T, NE])
        kmax = sb("kmax", [P, T])
        oh = sb("oh", [P, T, NE], bf16)
        psum_e = sb("psum_e", [P, T])
        gate = sb("gate", [P, T])
        ncnt = sb("ncnt", [P, NE])
        cnt = sb("cnt", [P, NE])
        cm = sb("cm", [P, NE, NE])
        sx = sb("sx", [P, NE])
        send = sb("send", [P, NE])
        ek_c = sb("ek_c", [P, NT, NE])
        eidf = sb("eidf", [P, NT])
        eid = sb("eid", [P, NT], i32)
        v3 = sb("v3", [P, T, NE])
        pos = sb("pos", [P, T])
        qf = sb("qf", [P, T])
        rf = sb("rf", [P, T])
        empty = sb("empty", [P, NT])
        inq = sb("inq", [P, T, NT], f16)
        inqt = sb("inqt", [P, T, NT], f16)
        inr = sb("inr", [P, T, P], f16)
        srcu = sb("srcu", [P, NT], u32)
        dstu = sb("dstu", [P, NT], u32)
        Xg = sb("Xg", [P, UNROLL, D])
        ewc_own = sb("ewc_own", [P, UNROLL - 4, EW])
        xT = sb("xT", [D, RING, P])
        hT = sb("hT", [P, RING, F])
        ysb = sb("ysb", [P, NT, D])
        Yg = xnT
        h1 = sb("h1", [P, 2, GT, D])
        h1T = sb("h1T", [D, 2, S])
        eq = sb("eq", [D, 2, S])
        rq = sb("rq", [D, 2, S])
        phiq = sb("phiq", [D, 2, S])
        ek = sb("ek", [P, 2, GT, D])
        rk = sb("rk", [P, 2, GT, D])
        phik = sb("phik", [P, 2, GT, D])
        vx = sb("vx", [P, 2, GT, D + 1])
        KVm = sb("KVm", [P, 2, D + H])
        den = sb("den", [P, 2, GT, H])
        rden = sb("rden", [P, 2, GT, H])
        att = sb("att", [P, 2, GT, D])
        attT = sb("attT", [D, 2, S])
        qa = ysb[:, 0:FC * S // D, :].rearrange("p (c a) d -> p c (a d)", c=FC)
        qb = sb("qb", [P, FC, S])
        actT = sb("actT", [P, 2, FC, S])
        gelu_bias = sb("gelu_bias", [P, 1])
        act_flat, qb_flat = actT.rearrange("p s c n -> p (s c n)"), qb.rearrange("p c n -> p (c n)")
        ewc = ([ewc_own[:, u, :] for u in range(UNROLL - 4)]
               + [act_flat[:, u * EW:(u + 1) * EW] for u in range(3)] + [qb_flat[:, 0:EW]])

        bank = [ctx.enter_context(nc.psum_tensor(f"bank{i}", [P, 512], f32)) for i in range(8)]

        x_in = [sem(f"x_in{g}") for g in range(NG)]
        rw_in = sem("rw_in")
        eb_in = sem("eb_in")
        w_in = sem("w_in")
        ew_in = sem("ew_in")
        const_ready = sem("const_ready")
        pool_chain = sem("pool_chain")
        dve_chain = sem("dve_chain")
        ebias_ready = sem("ebias_ready")
        eb1_T = sem("eb1_T")
        stats_ready = sem("stats_ready")
        rstd_ready = sem("rstd_ready")
        rstd0_ready = sem("rstd0_ready")
        xn_ready = sem("xn_ready")
        xn_by_act = sem("xn_by_act")
        xn_stored = sem("xn_stored")
        xnT_ps = sem("xnT_ps")
        xnT_ready = sem("xnT_ready")
        logits_ps = sem("logits_ps")
        lg_ready = sem("lg_ready")
        ex_ready = sem("ex_ready")
        oh_ready = sem("oh_ready")
        rank_ps = sem("rank_ps")
        eid_ready = sem("eid_ready")
        inq_ready = sem("inq_ready")
        inqt_ready = sem("inqt_ready")
        inr_ready = sem("inr_ready")
        src_ps = sem("src_ps")
        src_ready = sem("src_ready")
        dst_ready = sem("dst_ready")
        g_in = [sem(f"g_in{u}") for u in range(UNROLL)]
        ewc_in = [sem(f"ewc_in{u}") for u in range(UNROLL)]
        xg_T = sem("xg_T")
        xT_ready = sem("xT_ready")
        h_ps = sem("h_ps")
        hT_ready = sem("hT_ready")
        y_ps = sem("y_ps")
        y_ready = sem("y_ready")
        y_scattered = sem("y_scattered")
        yg_in = [sem(f"yg_in{g}") for g in range(NG)]
        combined = sem("combined")
        h1_ready = sem("h1_ready")
        h1_half_ready = sem("h1_half_ready")
        h1T_ps = sem("h1T_ps")
        h1T_ready = sem("h1T_ready")
        q_ps = sem("q_ps")
        k_ps = sem("k_ps")
        v_ps = sem("v_ps")
        q_out = sem("q_out")
        k_out = sem("k_out")
        v_out = sem("v_out")
        xi_ready = sem("xi_ready")
        phiq_ready = sem("phiq_ready")
        phik_ready = sem("phik_ready")
        ones_ready = sem("ones_ready")
        kvsum_ps = sem("kvsum_ps")
        KVm_ready = sem("KVm_ready")
        num_ps = sem("num_ps")
        att_ready = sem("att_ready")
        attT_ps = sem("attT_ps")
        attT_ready = sem("attT_ready")
        wo_ps = sem("wo_ps")
        x2_ready = sem("x2_ready")
        h2_ready = sem("h2_ready")
        h2T_ps = sem("h2T_ps")
        h2T_ready = sem("h2T_ready")
        u_ps = sem("u_ps")
        qa_ready = sem("qa_ready")
        qb_ready = sem("qb_ready")
        act_ready = sem("act_ready")
        w2_ps = sem("w2_ps")
        x3_ready = sem("x3_ready")
        res_ready = sem("res_ready")
        out_ready = sem("out_ready")
        out_by_pool = sem("out_by_pool")
        out_done = sem("out_done")

        PICKS = [[(0, 2), (2, 2)], [(g, 1) for g in range(NG)]]

        def picks(m, g=NG - 1):
            return m * len(PICKS[0]) + 1 + [first + n > g for first, n in PICKS[m]].index(True)

        LN = [(kind, b) for kind in ("m0", "a", "l", "m1") for b in range(B)]
        LN_AT = {k: i + 1 for i, k in enumerate(LN)}
        LOOPS = (NT - 3) // UNROLL

        def uses(ahead):
            return len(range(ahead, NT, UNROLL))

        class Tile:

            def __init__(self, i, n):
                self.k, self.parity, self.slot = i * UNROLL + n, n % 2, n % RING
                self.ahead, self.round = n % UNROLL, i + n // UNROLL

        def expert_tiles(eng, step, tiles=NT):
            loops = min(LOOPS, tiles // UNROLL)
            with eng.Fori(0, loops) as i:
                for n in range(UNROLL):
                    step(i, n)
            for k in range(loops * UNROLL, tiles):
                step(loops, k - loops * UNROLL)

        def left(i, n):
            return not isinstance(i, int) or i * UNROLL + n < NT

        def wait_xn(eng, m, g):
            before = sum(LAST_BY_ACT[:m])
            if g < LAST_BY_ACT[m]:
                eng.wait_ge(xn_by_act, before + g + 1)
            else:
                eng.wait_ge(xn_ready, m * NG - before + g + 1 - LAST_BY_ACT[m])

        def xn_bank(m, g):
            return 1 if m else g % 2

        def logits_bank(m, g):
            return 5 if m or g < 2 else 6

        block = ctx.enter_context(nc.Block())

        @block.sync
        def _(sp):
            for g in range(NG):
                sp.dma_start(x[:, g * GT:(g + 1) * GT, :], x_v[:, g * GT:(g + 1) * GT, :]).then_inc(x_in[g], 16)
            sp.dma_start(rw[:, :], rw_d).then_inc(rw_in, 16)
            sp.dma_start(rb[:, :], rb_d.unsqueeze(0).broadcast_to([P, NE])).then_inc(rw_in, 16)
            sp.dma_start(eb1r[:, :], eb1_d.rearrange("e (c p) -> (e c) p", p=P)).then_inc(eb_in, 16)
            sp.dma_start(ew[:, :, B2_AT:EW], eb2_d.unsqueeze(0).broadcast_to([P, NE, D])).then_inc(ew_in, 16)
            sp.dma_start(ew[:, :, W1_AT:W1_AT + F], ew1_d.rearrange("e p f -> p e f")).then_inc(ew_in, 16)
            for e in range(NE):
                sp.dma_start(ew[:, e, W2_AT:B1_AT].rearrange("p (c d) -> p c d", d=D),
                             ew2_d[e, :, :].rearrange("(c p) d -> p c d", p=P)).then_inc(ew_in, 16)
            for dst, src in ((wq[:, :], wq_d), (wkv[:, 0:D], wk_d), (wkv[:, D:2 * D], wv_d), (wo[:, :], wo_d),
                             (w1[:, :], w1_d), (w2[:, :, :], w2_d.rearrange("(c p) d -> p c d", p=P))):
                sp.dma_start(dst, src).then_inc(w_in, 16)
            for j, v in enumerate((g1_d, b1_d, g2_d, b2_d)):
                sp.dma_start(gb[:, j:j + 1], v.rearrange("(d a) -> d a", a=1)).then_inc(w_in, 16)
            for m in range(2):
                for g in range(NG):
                    wait_xn(sp, m, g)
                    sp.dma_start(xn_scr_v[:, g * GT:(g + 1) * GT, :],
                                 xn[:, g * GT:(g + 1) * GT, :]).then_inc(xn_stored, 16)

                def expert(t):
                    return sp.value_load(eid[0:1, bass.ds(t.k, 1)], min_val=0, max_val=NE - 1)

                def load_weights(t, e):
                    sp.dma_start(ewc[t.ahead], ew[:, bass.ds(e, 1), :].squeeze(1)).then_inc(ewc_in[t.ahead], 16)

                sp.wait_ge(eid_ready, m + 1)
                if m == 0:
                    sp.wait_ge(ew_in, 16 * (2 + NE))
                    sp.wait_ge(ebias_ready, 1)
                for k in range(UNROLL):
                    if k == FIRST:
                        sp.wait_ge(src_ready, m + 1)
                    load_weights(Tile(0, k), expert(Tile(0, k)))

                def step(i, n):
                    done, t = Tile(i, n), Tile(i, n + UNROLL)
                    e = expert(t)
                    sp.wait_ge(y_ready, m * NT + 1 + done.k)
                    load_weights(t, e)
                expert_tiles(sp, step, NT - UNROLL)
                sp.wait_ge(y_scattered, 16 * NT * (m + 1))
                for g in range(NG):
                    sp.dma_start(Yg[:, g * GT:(g + 1) * GT, :],
                                 y_scr_v[:, g * GT:(g + 1) * GT, :]).then_inc(yg_in[g], 16)
            for n, g in enumerate([g for g in range(NG) if g != POOL_GROUP] + [POOL_GROUP]):
                if g == POOL_GROUP:
                    sp.wait_ge(out_by_pool, 1)
                else:
                    sp.wait_ge(out_ready, n + 1)
                sp.dma_start(out_v[:, g * GT:(g + 1) * GT, :], x[:, g * GT:(g + 1) * GT, :]).then_inc(out_done, 16)
            sp.wait_ge(out_done, 16 * NG)

        @block.gpsimd
        def _(pool):
            chain = [0]

            def link(ins):
                chain[0] += 1
                ins.then_inc(pool_chain, 1)
                pool.wait_ge(pool_chain, chain[0])

            g = nc.gpsimd
            g.memset(ident[:, :], 0.0).then_inc(pool_chain, 1)
            g.memset(ones_bf[:, :], 1.0).then_inc(pool_chain, 1)
            g.memset(bmask[:, :, :], 1.0).then_inc(pool_chain, 1)
            g.memset(hmask[:, :], 1.0).then_inc(pool_chain, 1)
            g.memset(ltE[:, :, :], 1.0).then_inc(pool_chain, 1)
            g.memset(before[:, :], 1.0).then_inc(pool_chain, 1)
            chain[0] += 6
            g.memset(mhalf[:, :, :], -0.5).then_inc(const_ready, 1)
            pool.wait_ge(pool_chain, chain[0])
            g.affine_select(out=ident[:, :], in_=ident[:, :], compare_op=ALU.not_equal, fill=1.0, base=0,
                            pattern=[[-1, P]], channel_multiplier=1).then_inc(const_ready, 1)

            def normaliser(at):
                kind, n = LN[at]
                pool.wait_ge(stats_ready, at + 1)
                a, ts = at % 2, slice(n * GT, (n + 1) * GT)
                v = mv[:, ts, 1:2]
                g.tensor_scalar(vin[:, a, :, 0:1], v, 1.0, EPS, ALU.mult, ALU.add).then_inc(pool_chain, 1)
                chain[0] += 1
                if kind == "l" or kind == "m0" and n < LAST_BY_ACT[0] or kind == "m1" and n < LAST_BY_ACT[1]:
                    g.tensor_scalar(nmean[:, a, :, :], mv[:, ts, 0:1], -1.0, None, ALU.mult).then_inc(pool_chain, 1)
                    chain[0] += 1
                    pool.wait_ge(pool_chain, chain[0])
                    link(g.tensor_tensor(out=rstd[:, ts, 0:1], in0=vin[:, a, :, 0:1], in1=mhalf[:, :, 0:1], op=ALU.pow))
                    g.tensor_tensor(out=shift[:, ts, 0:1], in0=rstd[:, ts, 0:1], in1=nmean[:, a, :, :],
                                    op=ALU.mult).then_inc(rstd_ready, 1)
                    return
                if kind != "a":
                    pool.wait_ge(pool_chain, chain[0])
                    g.tensor_tensor(out=rstd[:, ts, 0:1], in0=vin[:, a, :, 0:1], in1=mhalf[:, :, 0:1], op=ALU.pow
                                    ).then_inc(rstd_ready, 1)
                    return
                g.tensor_scalar(vin[:, a, :, 1:2], v, 1.0 + EPS, EPS * EPS, ALU.mult, ALU.add).then_inc(pool_chain, 1)
                g.tensor_scalar(nmean[:, a, :, :], mv[:, ts, 0:1], -1.0, None, ALU.mult).then_inc(pool_chain, 1)
                chain[0] += 2
                pool.wait_ge(pool_chain, chain[0])
                for f, done in ((1, rstd_ready), (0, rstd0_ready)):
                    link(g.tensor_tensor(out=rstd[:, ts, f:f + 1], in0=vin[:, a, :, f:f + 1], in1=mhalf[:, :, f:f + 1],
                                         op=ALU.pow))
                    g.tensor_tensor(out=shift[:, ts, f:f + 1], in0=rstd[:, ts, f:f + 1], in1=nmean[:, a, :, :],
                                    op=ALU.mult).then_inc(done, 1)

            pool.wait_ge(const_ready, 2)
            for at in range(NG):
                normaliser(at)
            g.affine_select(out=before[:, :], in_=before[:, :], compare_op=ALU.is_gt, fill=0.0, base=0,
                            pattern=[[1, P]], channel_multiplier=-1).then_inc(const_ready, 1)
            g.affine_select(out=ltE[:, :, :], in_=ltE[:, :, :], compare_op=ALU.is_gt, fill=0.0, base=0,
                            pattern=[[1, NE], [-1, NE]], channel_multiplier=0).then_inc(const_ready, 1)
            g.iota(prefer[:, :], [[-1, NE]], base=NE, channel_multiplier=0,
                   allow_small_or_imprecise_dtypes=True).then_inc(const_ready, 1)
            g.iota(rowid[:, :], [[1, P]], base=0, channel_multiplier=0,
                   allow_small_or_imprecise_dtypes=True).then_inc(const_ready, 1)
            g.iota(tileid[:, :], [[1, NT]], base=0, channel_multiplier=0,
                   allow_small_or_imprecise_dtypes=True).then_inc(const_ready, 1)
            link(g.iota(token1[:, :], [[P, T]], base=1, channel_multiplier=1,
                   allow_small_or_imprecise_dtypes=True))
            g.iota(padrow[:, :], [[P, NT]], base=TOK + 1, channel_multiplier=1,
                   allow_small_or_imprecise_dtypes=True).then_inc(const_ready, 1)
            for m_, pat in ((bmask[:, :, :], [[-DH, H], [0, DH]]), (hmask[:, :], [[-DH, H]])):
                link(g.affine_select(out=m_, in_=m_, compare_op=ALU.is_ge, fill=0.0, base=0,
                                     pattern=pat, channel_multiplier=1))
                g.affine_select(out=m_, in_=m_, compare_op=ALU.is_ge, fill=0.0, base=DH - 1,
                                pattern=[[-s_, n_] for s_, n_ in pat], channel_multiplier=-1).then_inc(const_ready, 1)
            g.memset(gelu_bias[:, :], -0.1 * HALF).then_inc(const_ready, 1)
            g.memset(vx[:, :, :, D:D + 1], 1.0).then_inc(ones_ready, 1)

            def move_rows(m):
                def gather(k):
                    if k >= UNROLL:
                        pool.wait_ge(xg_T, m * NT + k - UNROLL + 1)
                    g.indirect_dma_start(out=Xg[:, k % UNROLL, :], out_offset=None, in_=xn_scr,
                                         in_offset=bass.IndirectOffsetOnAxis(ap=srcu[:, k:k + 1], axis=0)
                                         ).then_inc(g_in[k % UNROLL], 16)

                def scatter(k):
                    pool.wait_ge(y_ready, m * NT + k + 1)
                    g.indirect_dma_start(out=y_scr, out_offset=bass.IndirectOffsetOnAxis(ap=dstu[:, k:k + 1], axis=0),
                                         in_=ysb[:, k, :], in_offset=None).then_inc(y_scattered, 16)

                pool.wait_ge(inq_ready, m + 1)
                g.tensor_tensor(out=inqt[:, :, :], in0=inq[:, :, :], in1=bc(token1[:, :].unsqueeze(2), [P, T, NT]),
                                op=ALU.mult).then_inc(inqt_ready, 1)
                pool.wait_ge(xn_stored, 16 * NG * (m + 1))
                pool.wait_ge(src_ready, m + 1)
                for k in range(AHEAD):
                    gather(k)
                pool.wait_ge(dst_ready, m + 1)
                for k in range(NT):
                    scatter(k)
                    if k + AHEAD < NT:
                        gather(k + AHEAD)

            def combine(m, group, done):
                pool.wait_ge(yg_in[group], 16 * (m + 1))
                ts = slice(group * GT, (group + 1) * GT)
                link(g.tensor_tensor(out=Yg[:, ts, :], in0=Yg[:, ts, :], in1=bc(gate[:, ts].unsqueeze(2), [P, GT, D]),
                                     op=ALU.mult))
                g.tensor_tensor(out=x[:, ts, :], in0=Yg[:, ts, :], in1=x[:, ts, :], op=ALU.add).then_inc(done, 1)

            def residuals(b):
                pool.wait_ge(h2_ready, b + 1)
                g.tensor_tensor(out=xi[:, b * GT:(b + 1) * GT, :], in0=xi[:, b * GT:(b + 1) * GT, :],
                                in1=x[:, b * GT:(b + 1) * GT, :], op=ALU.add).then_inc(res_ready, 1)

            move_rows(0)
            for at in range(NG, NG + 2 * B):
                if at == NG + 2:
                    combine(0, 2, combined)
                    combine(0, 3, combined)
                normaliser(at)
            residuals(0)
            for b in range(B):
                if b + 1 < B:
                    residuals(b + 1)
                normaliser(LN_AT["m1", b] - 1)
            move_rows(1)
            combine(1, POOL_GROUP, out_by_pool)

        @block.scalar
        def _(act):
            A = nc.scalar.activation

            def take_xn(m, g):
                act.wait_ge(xnT_ps, m * NG + g + 1)
                A(xnT[:, g * GT:(g + 1) * GT, :], bank[xn_bank(m, g)][:, :], ACT.Copy).then_inc(xnT_ready, 1)

            def exponentials(m):
                act.wait_ge(lg_ready, picks(m))
                A(ex[:, :, :], lg[:, :, :], ACT.Exp).then_inc(ex_ready, 1)

            def experts(m):
                def step(i, n):
                    t = Tile(i, n)
                    act.wait_ge(h_ps, m * NT + 1 + t.k)
                    for c in range(FC):
                        last = A(hT[:, t.slot, c * P:(c + 1) * P], bank[2 + t.parity][:, c * P:(c + 1) * P],
                                 ACT.Relu, bias=ewc[t.ahead][:, B1_AT + c:B1_AT + c + 1])
                    last.then_inc(hT_ready, 1)
                expert_tiles(act, step)

            def renormalise(m, g):
                act.wait_ge(rstd_ready, LN_AT[f"m{m}", g])
                for t in range(g * GT, (g + 1) * GT):
                    last = A(xn[:, t, :], x[:, t, :], ACT.Identity, scale=rstd[:, t, 0:1], bias=shift[:, t, 0:1])
                last.then_inc(xn_by_act, 1)

            for g in range(LAST_BY_ACT[0]):
                renormalise(0, g)
            for g in range(NG):
                take_xn(0, g)
            exponentials(0)
            experts(0)
            act.wait_ge(w_in, 16 * 10)
            act.wait_ge(ones_ready, 1)

            def norm1(b):
                act.wait_ge(h1T_ps, b + 1)
                A(h1T[:, b % 2, :], bank[0][:, :], ACT.Identity, scale=gb[:, 0:1], bias=gb[:, 1:2]
                  ).then_inc(h1T_ready, 1)

            def normal1(b):
                act.wait_ge(rstd_ready, LN_AT["a", b])
                for t in range(b * GT, (b + 1) * GT if b else GT // 2):
                    last = A(h1[:, b % 2, t % GT, :], x[:, t, :], ACT.Identity, scale=rstd[:, t, 1:2], bias=shift[:, t, 1:2])
                last.then_inc(h1_ready, 1)

            def attention_input(b):
                act.wait_ge(rstd0_ready, b + 1)
                for t in range(b * GT, (b + 1) * GT):
                    last = A(xi[:, t, :], x[:, t, :], ACT.Identity, scale=rstd[:, t, 0:1], bias=shift[:, t, 0:1])
                last.then_inc(xi_ready, 1)

            def take_kv(b):
                s = b % 2
                act.wait_ge(k_ps, b + 1)
                A(ek[:, s, :, :], bank[3][:, :].rearrange("p (t d) -> p t d", d=D), ACT.Exp)
                A(rk[:, s, :, :], bank[3][:, :].rearrange("p (t d) -> p t d", d=D), ACT.Relu).then_inc(k_out, 1)
                act.wait_ge(v_ps, b + 1)
                A(vx[:, s, :, 0:D], bank[4][:, :].rearrange("p (t d) -> p t d", d=D), ACT.Copy).then_inc(v_out, 1)

            def take_q(b):
                s = b % 2
                act.wait_ge(q_ps, b + 1)
                A(eq[:, s, :], bank[2][:, :], ACT.Exp)
                A(rq[:, s, :], bank[2][:, :], ACT.Relu).then_inc(q_out, 1)

            def normal2(b):
                act.wait_ge(rstd_ready, LN_AT["l", b])
                for t in range(b * GT, (b + 1) * GT):
                    last = A(h1[:, b % 2, t % GT, :], xi[:, t, :], ACT.Identity, scale=rstd[:, t, 0:1], bias=shift[:, t, 0:1])
                last.then_inc(h2_ready, 1)

            def norm2(b):
                act.wait_ge(h2T_ps, b + 1)
                A(h1T[:, b % 2, :], bank[0][:, :], ACT.Identity, scale=gb[:, 2:3], bias=gb[:, 3:4]
                  ).then_inc(h2T_ready, 1)

            def lookup(b, chunks=range(FC)):
                for c in chunks:
                    act.wait_ge(qb_ready, b * FC + c + 1)
                    level = qb[:, c, :].bitcast(i16).rearrange("p (n two) -> p n two", two=2)[:, :, 0]
                    A(actT[:, b % 2, c, :], level, ACT.Gelu_apprx_tanh, scale=0.1,
                      bias=gelu_bias[:, 0:1]).then_inc(act_ready, 1)

            normal1(0)
            norm1(0)
            normal1(1)
            take_kv(0)
            take_q(0)
            for b in range(B):
                if b + 1 < B:
                    norm1(b + 1)
                if b == 0:
                    attention_input(0)
                if b + 1 < B:
                    if b + 2 < B:
                        normal1(b + 2)
                    take_kv(b + 1)
                else:
                    norm2(0)
                    normal2(1)
                act.wait_ge(attT_ps, b + 1)
                A(attT[:, b % 2, :], bank[1][:, :], ACT.Copy).then_inc(attT_ready, 1)
                if b + 1 < B:
                    take_q(b + 1)
                    attention_input(b + 1)
                if b + 2 == B:
                    normal2(0)

            norm2(1)
            lookup(0)
            for b in range(B):
                if b + 2 < B:
                    normal2(b + 2)
                if b + 1 < B:
                    lookup(b + 1, range(2))
                if b + 2 < B:
                    norm2(b + 2)
                if b >= 1:
                    renormalise(1, b - 1)
                if b + 1 < B:
                    lookup(b + 1, range(2, FC))
                if b >= 1:
                    take_xn(1, b - 1)
            take_xn(1, NG - 1)
            exponentials(1)
            experts(1)

        @block.tensor
        def _(pe):
            mm = nc.tensor.matmul

            def keep_warm(n):
                for _ in range(n):
                    mm(bank[2][:, :], ones_bf[:, :], bc(ones_bf[:, :].unsqueeze(1), [P, 4, P]), start=True, stop=True)

            pe.wait_ge(const_ready, 2)
            keep_warm(WARM_START)
            pe.wait_ge(eb_in, 16)
            nc.tensor.transpose(bank[7][:, 0:NE * FC], eb1r[:, :], ident[0:NE * FC, 0:NE * FC]).then_inc(eb1_T, 1)
            keep_warm(WARM_FRONT)
            pe.wait_ge(rw_in, 32)

            def turn_xn(m, g):
                wait_xn(pe, m, g)
                if g >= 2 - m:
                    pe.wait_ge(xnT_ready, m * NG + g - 1 + m)
                for j in range(GT):
                    last = nc.tensor.transpose(bank[xn_bank(m, g)][:, j * P:(j + 1) * P], xn[:, g * GT + j, :],
                                               ident[:, :])
                last.then_inc(xnT_ps, 1)

            def logits(m, g):
                pe.wait_ge(xnT_ready, m * NG + g + 1)
                if m == 1 and g >= 1:
                    pe.wait_ge(lg_ready, picks(m, g - 1))
                at = 0 if m else g % 2 * GT
                for j in range(GT):
                    last = mm(bank[logits_bank(m, g)][:, (at + j) * NE:(at + j + 1) * NE], xnT[:, g * GT + j, :], rw[:, :], start=True, stop=True)
                last.then_inc(logits_ps, 1)

            def ranks(m):
                R = bank[3]
                pe.wait_ge(oh_ready, picks(m))
                pe.wait_ge(const_ready, 11)

                def spread(t):
                    n = T - t
                    return bc(oh[:, t, :].unsqueeze(1), [P, n, NE])

                mm(R[:, NE:(T + 1) * NE], ones_bf[:, :], spread(0), start=True, stop=False, skip_group_check=True)
                mm(R[:, 0:NE], before[:, :], oh[:, 0, :], start=False, stop=False, skip_group_check=True)
                mm(R[:, NE:T * NE], before[:, :], oh[:, 1:T, :], start=False, stop=False, skip_group_check=True)
                for t in range(1, T):
                    last = mm(R[:, (t + 1) * NE:(T + 1) * NE], ones_bf[:, :], spread(t),
                              start=False, stop=t == T - 1, skip_group_check=True)
                last.then_inc(rank_ps, 1)

            def sources(m):
                pe.wait_ge(inqt_ready, m + 1)
                for t in range(T):
                    pe.wait_ge(inr_ready, m * T + t + 1)
                    last = mm(bank[4][:, 0:NT], inr[:, t, :], inqt[:, t, :], start=t == 0, stop=t == T - 1)
                last.then_inc(src_ps, 1)

            def experts(m):
                def turn(i, n):
                    t = Tile(i, n)
                    pe.wait_ge(g_in[t.ahead], 16 * (m * uses(t.ahead) + 1 + t.round))
                    nc.tensor.transpose(bank[t.parity][:, 0:P], Xg[:, t.ahead, :], ident[:, :]).then_inc(xg_T, 1)

                def up(i, n):
                    t = Tile(i, n)
                    pe.wait_ge(ewc_in[t.ahead], 16 * (m * uses(t.ahead) + 1 + t.round))
                    pe.wait_ge(xT_ready, m * NT + 1 + t.k)
                    for c in range(FC):
                        last = mm(bank[2 + t.parity][:, c * P:(c + 1) * P], ewc[t.ahead][:, c * P:(c + 1) * P],
                                  xT[:, t.slot, :], start=True, stop=True)
                    last.then_inc(h_ps, 1)

                def down(i, n):
                    t = Tile(i, n)
                    pe.wait_ge(hT_ready, m * NT + 1 + t.k)
                    if not left(i, n + 1):
                        pe.wait_ge(y_ready, m * NT + t.k - 1)
                    for c in range(FC):
                        last = mm(bank[4 + t.parity][:, 0:D], hT[:, t.slot, c * P:(c + 1) * P],
                                  ewc[t.ahead][:, W2_AT + c * D:W2_AT + (c + 1) * D], start=c == 0, stop=c == FC - 1)
                    last.then_inc(y_ps, 1)

                turn(0, 0)
                turn(0, 1)
                up(0, 0)

                def step(i, n):
                    if left(i, n + 2):
                        turn(i, n + 2)
                    if left(i, n + 1):
                        up(i, n + 1)
                    down(i, n)
                expert_tiles(pe, step)

            turn_xn(0, 0)
            for g in range(NG):
                keep_warm(2)
                if g + 1 < NG:
                    turn_xn(0, g + 1)
                logits(0, g)
            keep_warm(4)
            ranks(0)
            keep_warm(WARM_ROUTE)
            sources(0)
            keep_warm(WARM_GATHER)
            experts(0)
            pe.wait_ge(w_in, 16 * 10)
            keep_warm(WARM_STEP)
            pe.wait_ge(y_ready, NT)
            keep_warm(WARM_STEP)
            pe.wait_ge(y_scattered, 16 * NT)
            keep_warm(WARM_STEP)
            pe.wait_ge(yg_in[0], 16)
            keep_warm(WARM_STEP)
            pe.wait_ge(yg_in[NG - 1], 16)
            keep_warm(WARM_STEP)
            pe.wait_ge(stats_ready, LN_AT["a", 0])
            keep_warm(WARM_STEP)
            pe.wait_ge(rstd_ready, LN_AT["a", 0])
            keep_warm(WARM_STEP // 2)

            def turn1(b):
                pe.wait_ge(h1_ready, b + 1)
                if b == 0:
                    pe.wait_ge(h1_half_ready, 1)
                for j in range(GT):
                    last = nc.tensor.transpose(bank[0][:, j * P:(j + 1) * P], h1[:, b % 2, j, :], ident[:, :])
                last.then_inc(h1T_ps, 1)

            def keys_values(b):
                pe.wait_ge(h1T_ready, b + 1)
                if b >= 1:
                    pe.wait_ge(v_out, b)
                for bk, at, done in ((3, 0, k_ps), (4, D, v_ps)):
                    for j in range(GT):
                        last = mm(bank[bk][:, j * D:(j + 1) * D], h1T[:, b % 2, j * P:(j + 1) * P],
                                  wkv[:, at:at + D], start=True, stop=True)
                    last.then_inc(done, 1)

            def queries(b):
                if b >= 1:
                    pe.wait_ge(q_out, b)
                mm(bank[2][:, :], wq[:, :], h1T[:, b % 2, :], start=True, stop=True).then_inc(q_ps, 1)

            def sum_kv(b):
                s = b % 2
                pe.wait_ge(phik_ready, b + 1)
                pe.wait_ge(v_out, b + 1)
                for j in range(GT):
                    last = mm(bank[5][:, 0:D + 1], phik[:, s, j, :], vx[:, s, j, :], start=j == 0, stop=j == GT - 1)
                last.then_inc(kvsum_ps, 1)

            def numerators(b):
                s = b % 2
                pe.wait_ge(KVm_ready, b + 1)
                pe.wait_ge(phiq_ready, b + 1)
                if b >= 1:
                    pe.wait_ge(x2_ready, b)
                for j in range(GT):
                    last = mm(bank[6 + j // 2][:, (j % 2) * (D + H):(j % 2 + 1) * (D + H)],
                              phiq[:, s, j * P:(j + 1) * P], KVm[:, s, :], start=True, stop=True)
                last.then_inc(num_ps, 1)

            def turn_att(b):
                pe.wait_ge(att_ready, b + 1)
                for j in range(GT):
                    last = nc.tensor.transpose(bank[1][:, j * P:(j + 1) * P], att[:, b % 2, j, :], ident[:, :])
                last.then_inc(attT_ps, 1)

            def project(b):
                pe.wait_ge(attT_ready, b + 1)
                for j in range(GT):
                    last = mm(bank[6][:, j * P:(j + 1) * P], attT[:, b % 2, j * P:(j + 1) * P], wo[:, :],
                              start=True, stop=True)
                last.then_inc(wo_ps, 1)

            def turn2(b):
                pe.wait_ge(h2_ready, b + 1)
                if b >= 1:
                    pe.wait_ge(h2T_ready, b)
                for j in range(GT):
                    last = nc.tensor.transpose(bank[0][:, j * P:(j + 1) * P], h1[:, b % 2, j, :], ident[:, :])
                last.then_inc(h2T_ps, 1)

            def up2(b, chunks=range(FC)):
                pe.wait_ge(h2T_ready, b + 1)
                for c in chunks:
                    n = b * FC + c
                    if n >= 3:
                        pe.wait_ge(qa_ready, n - 2)
                    mm(bank[2 + n % 3][:, :], w1[:, c * P:(c + 1) * P], h1T[:, b % 2, :], start=True, stop=True
                       ).then_inc(u_ps, 1)

            def down2(b):
                if b >= 2:
                    pe.wait_ge(x3_ready, b - 1)
                pe.wait_ge(act_ready, (b + 1) * FC)
                for j in range(GT):
                    for c in range(FC):
                        last = mm(bank[6 + b % 2][:, j * P:(j + 1) * P], actT[:, b % 2, c, j * P:(j + 1) * P],
                                  w2[:, c, :], start=c == 0, stop=c == FC - 1)
                last.then_inc(w2_ps, 1)

            turn1(0)
            keys_values(0)
            queries(0)
            for b in range(B):
                more = b + 1 < B
                sum_kv(b)
                if more:
                    turn1(b + 1)
                numerators(b)
                if more:
                    keys_values(b + 1)
                else:
                    turn2(0)
                    up2(0, range(3))
                turn_att(b)
                if more:
                    queries(b + 1)
                else:
                    turn2(1)
                project(b)

            up2(0, range(3, FC))
            for b in range(B):
                if b + 1 < B:
                    up2(b + 1)
                if b + 2 < B:
                    turn2(b + 2)
                if b >= 2:
                    logits(1, b - 2)
                down2(b)
                if b >= 1:
                    turn_xn(1, b - 1)
            logits(1, NG - 2)
            keep_warm(WARM_TAIL)
            turn_xn(1, NG - 1)
            keep_warm(3)
            logits(1, NG - 1)
            keep_warm(4)
            ranks(1)
            keep_warm(WARM_ROUTE)
            sources(1)
            keep_warm(WARM_GATHER)
            experts(1)

        @block.vector
        def _(dve):
            chain = [0]
            v = nc.vector

            def link(ins):
                chain[0] += 1
                ins.then_inc(dve_chain, 1)
                dve.wait_ge(dve_chain, chain[0])

            def later(ins):
                chain[0] += 1
                ins.then_inc(dve_chain, 1)
                return chain[0]

            def statistics(kind, n, src):
                for j in range(GT):
                    last = v.bn_stats(stat[:, j, :], src[:, n * GT + j, :])
                link(last)
                for j in range(GT):
                    last = v.bn_aggr(mv[:, n * GT + j, :], stat[:, j, :])
                last.then_inc(stats_ready, 1)
                dve.wait_ge(stats_ready, LN_AT[kind, n])

            def normalise(dst, src, n):
                for j in range(GT):
                    t = n * GT + j
                    last = v.tensor_scalar(dst(j), src[:, t, :], mv[:, t, 0:1], rstd[:, t, 0:1],
                                           ALU.subtract, ALU.mult)
                return last

            def pick(m, g, n=1):
                ts, nt = slice(g * GT, (g + n) * GT), n * GT
                dve.wait_ge(logits_ps, m * NG + g + n)
                link(v.tensor_tensor(out=lg[:, ts, :],
                                     in0=bank[logits_bank(m, g)][:, 0:nt * NE].rearrange("p (t e) -> p t e", e=NE),
                                     in1=bc(rb[:, :].unsqueeze(1), [P, nt, NE]), op=ALU.add))
                link(v.tensor_reduce(lmax[:, ts], lg[:, ts, :], AX, ALU.max))
                v.tensor_tensor(out=lg[:, ts, :], in0=lg[:, ts, :], in1=bc(lmax[:, ts].unsqueeze(2), [P, nt, NE]),
                                op=ALU.subtract).then_inc(lg_ready, 1)
                dve.wait_ge(lg_ready, picks(m, g))
                if m == 0 and g == 0:
                    dve.wait_ge(const_ready, 11)
                link(v.scalar_tensor_tensor(out=key[:, ts, :], in0=lg[:, ts, :], scalar=0.0,
                                            in1=bc(prefer[:, :].unsqueeze(1), [P, nt, NE]),
                                            op0=ALU.is_ge, op1=ALU.mult))
                link(v.tensor_reduce(kmax[:, ts], key[:, ts, :], AX, ALU.max))
                v.tensor_tensor(out=oh[:, ts, :], in0=key[:, ts, :], in1=bc(kmax[:, ts].unsqueeze(2), [P, nt, NE]),
                                op=ALU.is_equal).then_inc(oh_ready, 1)

            def gates(m):
                dve.wait_ge(ex_ready, m + 1)
                link(v.tensor_reduce(psum_e[:, :], ex[:, :, :], AX, ALU.add))
                link(v.reciprocal(gate[:, :], psum_e[:, :]))
                link(v.tensor_scalar(gate[:, :], gate[:, :], 0.5, None, ALU.mult))

            def route(m):
                dve.wait_ge(oh_ready, picks(m))
                dve.wait_ge(rank_ps, m + 1)
                R = bank[3]
                link(v.tensor_scalar(ncnt[:, :], R[:, T * NE:(T + 1) * NE], 1.0 / P, (P - 1.0) / P - 0.498046875,
                                     ALU.mult, ALU.add))
                link(v.tensor_scalar(cnt[:, :], ncnt[:, :], MAGIC, MAGIC, ALU.add, ALU.subtract))
                link(v.tensor_tensor(out=cm[:, :, :], in0=bc(cnt[:, :].unsqueeze(1), [P, NE, NE]), in1=ltE[:, :, :],
                                     op=ALU.mult))
                link(v.tensor_reduce(sx[:, :], cm[:, :, :], AX, ALU.add))
                send_done = later(v.tensor_tensor(out=send[:, :], in0=sx[:, :], in1=cnt[:, :], op=ALU.add))
                v3_done = later(v.scalar_tensor_tensor(
                    out=v3[:, :, :], in0=bc(sx[:, :].unsqueeze(1), [P, T, NE]), scalar=float(P),
                    in1=R[:, 0:T * NE].rearrange("p (t e) -> p t e", e=NE), op0=ALU.mult, op1=ALU.add))
                dve.wait_ge(dve_chain, send_done)
                ek_done = later(v.tensor_tensor(out=ek_c[:, :, :], in0=bc(tileid[:, :].unsqueeze(2), [P, NT, NE]),
                                                in1=bc(send[:, :].unsqueeze(1), [P, NT, NE]), op=ALU.is_ge))
                dve.wait_ge(dve_chain, v3_done)
                v3_done = later(v.tensor_tensor(out=v3[:, :, :], in0=v3[:, :, :], in1=oh[:, :, :], op=ALU.mult))
                dve.wait_ge(dve_chain, ek_done)
                eid_done = later(v.tensor_reduce(eidf[:, :], ek_c[:, :, :], AX, ALU.add))
                dve.wait_ge(dve_chain, v3_done)
                pos_done = later(v.tensor_reduce(pos[:, :], v3[:, :, :], AX, ALU.add))
                dve.wait_ge(dve_chain, eid_done)
                v.tensor_scalar(eid[:, :], eidf[:, :], NE - 1.0, None, ALU.min).then_inc(eid_ready, 1)
                dve.wait_ge(dve_chain, pos_done)
                link(v.tensor_scalar(qf[:, :], pos[:, :], 1.0 / P, -0.498046875, ALU.mult, ALU.add))
                link(v.tensor_scalar(qf[:, :], qf[:, :], MAGIC, MAGIC, ALU.add, ALU.subtract))
                link(v.scalar_tensor_tensor(out=rf[:, :], in0=qf[:, :], scalar=-float(P), in1=pos[:, :],
                                            op0=ALU.mult, op1=ALU.add))
                v.tensor_tensor(out=inq[:, :, :], in0=bc(tileid[:, :].unsqueeze(1), [P, T, NT]),
                                in1=bc(qf[:, :].unsqueeze(2), [P, T, NT]), op=ALU.is_equal).then_inc(inq_ready, 1)
                for t in range(T):
                    v.tensor_scalar(inr[:, t, :], rowid[:, :], rf[:, t:t + 1], None, ALU.is_equal).then_inc(inr_ready, 1)
                dve.wait_ge(src_ps, m + 1)
                M = bank[4][:, 0:NT]
                v.tensor_scalar(srcu[:, :], M, 1.0, 0.0, ALU.subtract, ALU.max).then_inc(src_ready, 1)
                link(v.scalar_tensor_tensor(out=empty[:, :], in0=M, scalar=0.0, in1=padrow[:, :],
                                            op0=ALU.is_equal, op1=ALU.mult))
                v.scalar_tensor_tensor(out=dstu[:, :], in0=M, scalar=1.0, in1=empty[:, :],
                                       op0=ALU.subtract, op1=ALU.add).then_inc(dst_ready, 1)
                gates(m)

            def experts(m):
                def take_x(i, n):
                    t = Tile(i, n)
                    dve.wait_ge(xg_T, m * NT + 1 + t.k)
                    v.tensor_copy(xT[:, t.slot, :], bank[t.parity][:, 0:P]).then_inc(xT_ready, 1)

                def take_y(i, n):
                    t = Tile(i, n)
                    dve.wait_ge(y_ps, m * NT + 1 + t.k)
                    v.tensor_tensor(out=ysb[:, bass.ds(t.k, 1), :].squeeze(1), in0=bank[4 + t.parity][:, 0:D],
                                    in1=ewc[t.ahead][:, B2_AT:EW], op=ALU.add).then_inc(y_ready, 1)

                take_x(0, 0)
                take_x(0, 1)

                def step(i, n):
                    if left(i, n + 2):
                        take_x(i, n + 2)
                    take_y(i, n)
                expert_tiles(dve, step)

            def combine(m, g):
                dve.wait_ge(yg_in[g], 16 * (m + 1))
                for t in range(g * GT, (g + 1) * GT):
                    last = v.scalar_tensor_tensor(out=x[:, t, :], in0=Yg[:, t, :], scalar=gate[:, t:t + 1],
                                                  in1=x[:, t, :], op0=ALU.mult, op1=ALU.add)
                return last

            def begin0(g):
                dve.wait_ge(x_in[g], 16)
                statistics("m0", g, x)

            def renormalise(m, g):
                dve.wait_ge(rstd_ready, LN_AT[f"m{m}", g])
                normalise(lambda j: xn[:, g * GT + j, :], x, g).then_inc(xn_ready, 1)

            for g in range(NG):
                begin0(g)
            for g in range(LAST_BY_ACT[0], NG):
                renormalise(0, g)
            dve.wait_ge(eb1_T, 1)
            v.tensor_copy(ew[:, :, B1_AT:B2_AT], bank[7][:, 0:NE * FC].rearrange("p (e c) -> p e c", c=FC)
                          ).then_inc(ebias_ready, 1)
            for g, n in PICKS[0]:
                pick(0, g, n)
            route(0)
            experts(0)

            def begin(b):
                if b < 2:
                    link(combine(0, b))
                else:
                    dve.wait_ge(combined, b - 1)
                statistics("a", b, x)

            def phi(dst, e, r, done):
                v.scalar_tensor_tensor(out=dst, in0=e, scalar=1.0, in1=r, op0=ALU.min, op1=ALU.add).then_inc(done, 1)

            def phi_k(b):
                s = b % 2
                dve.wait_ge(k_out, b + 1)
                phi(phik[:, s, :, :], ek[:, s, :, :], rk[:, s, :, :], phik_ready)

            def phi_q(b):
                s = b % 2
                dve.wait_ge(q_out, b + 1)
                phi(phiq[:, s, :], eq[:, s, :], rq[:, s, :], phiq_ready)

            def mask_kv(b):
                s = b % 2
                dve.wait_ge(kvsum_ps, b + 1)
                v.tensor_tensor(out=KVm[:, s, 0:D], in0=bank[5][:, 0:D], in1=bmask[:, :, :].rearrange("p h e -> p (h e)"),
                                op=ALU.mult)
                v.tensor_scalar(KVm[:, s, D:D + H], hmask[:, :], bank[5][:, D:D + 1], None, ALU.mult
                                ).then_inc(KVm_ready, 1)

            def divide(b):
                s = b % 2
                dve.wait_ge(num_ps, b + 1)
                nd = [bank[6 + j][:, 0:2 * (D + H)].rearrange("p (t n) -> p t n", t=2) for j in range(2)]
                for j in range(2):
                    last = v.tensor_scalar(den[:, s, 2 * j:2 * j + 2, :], nd[j][:, :, D:D + H], 1e-6, None, ALU.add)
                link(last)
                link(v.reciprocal(rden[:, s, :, :], den[:, s, :, :]))
                for j in range(2):
                    ts = slice(2 * j, 2 * j + 2)
                    last = v.tensor_tensor(
                        out=att[:, s, ts, :].rearrange("p t (h e) -> p t h e", e=DH),
                        in0=nd[j][:, :, 0:D].rearrange("p t (h e) -> p t h e", e=DH),
                        in1=bc(rden[:, s, ts, :].unsqueeze(3), [P, 2, H, DH]), op=ALU.mult)
                last.then_inc(att_ready, 1)

            def residual(b):
                dve.wait_ge(wo_ps, b + 1)
                dve.wait_ge(xi_ready, b + 1)
                xb = xi[:, b * GT:(b + 1) * GT, :]
                v.tensor_tensor(out=xb, in0=bank[6][:, :].rearrange("p (t d) -> p t d", d=D), in1=xb, op=ALU.add
                                ).then_inc(x2_ready, 1)

            def begin2(b):
                dve.wait_ge(x2_ready, b + 1)
                statistics("l", b, xi)

            def quantise(b, chunks=range(FC)):
                for c in chunks:
                    n = b * FC + c
                    dve.wait_ge(u_ps, n + 1)
                    v.tensor_scalar(qa[:, c, :], bank[2 + n % 3][:, :], 10.0, QBASE + HALF, ALU.mult, ALU.add
                                    ).then_inc(qa_ready, 1)
                    dve.wait_ge(qa_ready, n + 1)
                    if b >= 1:
                        dve.wait_ge(act_ready, n - FC + 1)
                    v.tensor_scalar(qb[:, c, :], qa[:, c, :], QBASE, QBASE + LEVELS - 1, ALU.max, ALU.min
                                    ).then_inc(qb_ready, 1)

            begin(0)
            begin(1)
            dve.wait_ge(rstd_ready, LN_AT["a", 0])
            for t in range(GT // 2, GT):
                last = v.tensor_scalar(h1[:, 0, t, :], x[:, t, :], mv[:, t, 0:1], rstd[:, t, 1:2], ALU.subtract, ALU.mult)
            last.then_inc(h1_half_ready, 1)
            phi_k(0)
            begin(2)
            phi_q(0)
            for b in range(B):
                mask_kv(b)
                if b == 0:
                    begin(3)
                if b >= 1:
                    begin2(b - 1)
                divide(b)
                if b + 1 < B:
                    phi_k(b + 1)
                if b + 1 == B:
                    quantise(0, range(3))
                residual(b)
                if b + 1 < B:
                    phi_q(b + 1)
            begin2(B - 1)

            quantise(0, range(3, FC))
            for b in range(B):
                if b + 1 < B:
                    quantise(b + 1)
                if b >= 2:
                    pick(1, b - 2)
                dve.wait_ge(w2_ps, b + 1)
                dve.wait_ge(res_ready, b + 1)
                v.tensor_tensor(out=x[:, b * GT:(b + 1) * GT, :],
                                in0=bank[6 + b % 2][:, :].rearrange("p (t d) -> p t d", d=D),
                                in1=xi[:, b * GT:(b + 1) * GT, :], op=ALU.add).then_inc(x3_ready, 1)
                dve.wait_ge(x3_ready, b + 1)
                statistics("m1", b, x)
            pick(1, NG - 2)
            renormalise(1, NG - 1)
            pick(1, NG - 1)

            route(1)
            experts(1)
            for g in range(NG):
                if g != POOL_GROUP:
                    combine(1, g).then_inc(out_ready, 1)


_INS = ['L0_attn_x', 'L0_attn_ln1_g', 'L0_attn_ln1_b', 'L0_attn_wq', 'L0_attn_wk', 'L0_attn_wv', 'L0_attn_wo',
        'L0_attn_ln2_g', 'L0_attn_ln2_b', 'L0_attn_w1', 'L0_attn_w2', 'L0_ffn_router_W', 'L0_ffn_router_b',
        'L0_ffn_W1', 'L0_ffn_b1', 'L0_ffn_W2', 'L0_ffn_b2']
_OUTS = [((B, S, D), 'float32')]


def kernel(**inputs):
    import numpy as _np
    import concourse.bacc as _bacc
    from concourse import mybir as _mybir
    from concourse.bass_utils import run_bass_kernel_spmd as _run

    nc = _bacc.Bacc("TRN2", target_bir_lowering=False, num_devices=1)
    arrays, args = {}, []
    for name in _INS:
        a = _np.ascontiguousarray(inputs[name])
        arrays[f"in_{name}_dram"] = a
        args.append(nc.dram_tensor(f"in_{name}_dram", a.shape, _mybir.dt.from_np(a.dtype), kind="ExternalInput").ap())
    for i, (shape, dtype) in enumerate(_OUTS):
        dt = _mybir.dt.from_np(_np.dtype(dtype))
        args.append(nc.dram_tensor(f"out_{i}_dram", shape, dt, kind="ExternalOutput").ap())
    macaron_kernel(nc, *args)
    r = _run(nc, [arrays], core_ids=[0])
    got = tuple(r.results[0][f"out_{i}_dram"] for i in range(len(_OUTS)))
    return got[0]
```
